# Optimizing a Trainium2 kernel written in Bass

```python
import numpy as np
import jax
import jax.numpy as jnp

def _softmax(x, axis=-1):
    return jax.nn.softmax(x, axis=axis)

def _gelu(x):
    return jax.nn.gelu(x, approximate=True)

def _silu(x):
    return jax.nn.silu(x)

def _sigmoid(x):
    return jax.nn.sigmoid(x)

def _layernorm(x, axis=-1, eps=1e-05):
    m = jnp.mean(x, axis=axis, keepdims=True)
    v = jnp.var(x, axis=axis, keepdims=True)
    return (x - m) / jnp.sqrt(v + eps)

def _scatter_add(tgt, idx, src, axis=0):
    return tgt.at[idx].add(src)

def _segment_sum(src, seg, n):
    return jax.ops.segment_sum(src, seg, n)
kernel_name = 'mk_seq_preln_d1_jaxref_r8_791fb4'

def setup_inputs(seed: int=0):
    np.random.seed(seed)
    _w = jnp.asarray

    def _L0_attn_setup():
        import jax, jax.numpy as jnp
        import numpy as np
        EMBED_DIM = 128
        NUM_HEADS = 16
        HEAD_DIM = EMBED_DIM // NUM_HEADS
        key = jax.random.key(seed)
        kx, kq, kk, kv, ko = jax.random.split(key, 5)
        scale = 1.0 / np.sqrt(EMBED_DIM)
        return {'x': jax.random.normal(kx, (4, 256, EMBED_DIM), dtype=jnp.float32), 'w_q': jax.random.normal(kq, (EMBED_DIM, EMBED_DIM), dtype=jnp.float32) * scale, 'w_k': jax.random.normal(kk, (EMBED_DIM, EMBED_DIM), dtype=jnp.float32) * scale, 'w_v': jax.random.normal(kv, (EMBED_DIM, EMBED_DIM), dtype=jnp.float32) * scale, 'w_o': jax.random.normal(ko, (EMBED_DIM, EMBED_DIM), dtype=jnp.float32) * scale}
    _L0_attn_in = _L0_attn_setup()

    def _L0_ffn_setup():
        import jax, jax.numpy as jnp
        import numpy as np
        B, S, D, E, F, K = (4, 128, 128, 8, 352, 1)
        key = jax.random.key(seed)
        ks = jax.random.split(key, 8)
        sc = 0.02
        return {'x_bsD': jax.random.normal(ks[0], (B, S, D), jnp.float32), 'router_DE': jax.random.normal(ks[1], (D, E), jnp.float32) * sc, 'w1_eDF': jax.random.normal(ks[2], (E, D, F), jnp.float32) * sc, 'w3_eDF': jax.random.normal(ks[3], (E, D, F), jnp.float32) * sc, 'w2_eFD': jax.random.normal(ks[4], (E, F, D), jnp.float32) * sc, 'ws1_DF': jax.random.normal(ks[5], (D, F), jnp.float32) * sc, 'ws3_DF': jax.random.normal(ks[6], (D, F), jnp.float32) * sc, 'ws2_FD': jax.random.normal(ks[7], (F, D), jnp.float32) * sc}
    _L0_ffn_in = _L0_ffn_setup()
    _d = {'L0_attn_x': _L0_attn_in['x'], 'L0_attn_w_q': _L0_attn_in['w_q'], 'L0_attn_w_k': _L0_attn_in['w_k'], 'L0_attn_w_v': _L0_attn_in['w_v'], 'L0_attn_w_o': _L0_attn_in['w_o'], 'L0_ffn_router_DE': _L0_ffn_in['router_DE'], 'L0_ffn_w1_eDF': _L0_ffn_in['w1_eDF'], 'L0_ffn_w3_eDF': _L0_ffn_in['w3_eDF'], 'L0_ffn_w2_eFD': _L0_ffn_in['w2_eFD'], 'L0_ffn_ws1_DF': _L0_ffn_in['ws1_DF'], 'L0_ffn_ws3_DF': _L0_ffn_in['ws3_DF'], 'L0_ffn_ws2_FD': _L0_ffn_in['ws2_FD']}
    _x0 = _d['L0_attn_x']
    _d['L0_attn_x'] = jax.random.normal(jax.random.fold_in(jax.random.key(seed), 1), (4, 1024, 128), dtype=_x0.dtype)
    del _x0
    return _d

def reference(L0_attn_x, L0_attn_w_q, L0_attn_w_k, L0_attn_w_v, L0_attn_w_o, L0_ffn_router_DE, L0_ffn_w1_eDF, L0_ffn_w3_eDF, L0_ffn_w2_eFD, L0_ffn_ws1_DF, L0_ffn_ws3_DF, L0_ffn_ws2_FD):

    def _L0_attn_ref(x, w_q, w_k, w_v, w_o):
        import jax, jax.numpy as jnp
        import numpy as np
        EMBED_DIM = 128
        NUM_HEADS = 16
        HEAD_DIM = EMBED_DIM // NUM_HEADS
        b, s, _ = x.shape
        q = (x @ w_q.T).reshape(b, s, NUM_HEADS, HEAD_DIM).transpose(0, 2, 1, 3)
        k = (x @ w_k.T).reshape(b, s, NUM_HEADS, HEAD_DIM).transpose(0, 2, 1, 3)
        v = (x @ w_v.T).reshape(b, s, NUM_HEADS, HEAD_DIM).transpose(0, 2, 1, 3)
        scores = jnp.einsum('bhqd,bhkd->bhqk', q, k) / jnp.sqrt(jnp.float32(HEAD_DIM)).astype(x.dtype)
        attn = jax.nn.softmax(scores, axis=-1)
        out = jnp.einsum('bhqk,bhkd->bhqd', attn, v)
        out = out.transpose(0, 2, 1, 3).reshape(b, s, EMBED_DIM)
        return out @ w_o.T

    def _L0_ffn_ref(x_bsD, router_DE, w1_eDF, w3_eDF, w2_eFD, ws1_DF, ws3_DF, ws2_FD):
        import jax, jax.numpy as jnp
        import numpy as np
        B, S, D, E, F, K = (4, 128, 128, 8, 352, 1)
        b, s, d = x_bsD.shape
        a = b * s
        x_aD = x_bsD.reshape(a, d)
        scores_aE = x_aD @ router_DE
        vals_aK, idx_aK = jax.lax.top_k(scores_aE, K)
        masked_aE = jnp.full_like(scores_aE, -jnp.inf).at[jnp.arange(a)[:, None], idx_aK].set(vals_aK)
        gates_Ea = jax.nn.sigmoid(masked_aE).T
        routed_in_EaD = jax.lax.stop_gradient(gates_Ea[:, :, None] * x_aD[None, :, :])
        mid_EaF = jax.nn.silu(jnp.einsum('ead,edf->eaf', routed_in_EaD, w1_eDF)) * jnp.einsum('ead,edf->eaf', routed_in_EaD, w3_eDF)
        routed_out_EaD = jnp.einsum('eaf,efd->ead', mid_EaF, w2_eFD)
        shared_aD = jax.nn.silu(x_aD @ ws1_DF) * (x_aD @ ws3_DF) @ ws2_FD
        out_aD = shared_aD + routed_out_EaD.sum(axis=0)
        return out_aD.reshape(b, s, d)
    x = L0_attn_x
    x = x + _L0_attn_ref(_layernorm(x, axis=-1), L0_attn_w_q, L0_attn_w_k, L0_attn_w_v, L0_attn_w_o)
    x = x + _L0_ffn_ref(_layernorm(x, axis=-1), L0_ffn_router_DE, L0_ffn_w1_eDF, L0_ffn_w3_eDF, L0_ffn_w2_eFD, L0_ffn_ws1_DF, L0_ffn_ws3_DF, L0_ffn_ws2_FD)
    return x

_drawn_inputs = setup_inputs


def setup_inputs(seed=0):
    import zlib

    import numpy as np

    out = dict(_drawn_inputs(seed))
    spreads = {}
    factors = {'L0_ffn_router_DE': 8.0,
     'L0_ffn_w1_eDF': 8.0,
     'L0_ffn_w3_eDF': 8.0,
     'L0_ffn_w2_eFD': 8.0,
     'L0_ffn_ws1_DF': 5.869,
     'L0_ffn_ws3_DF': 5.863,
     'L0_ffn_ws2_FD': 5.865}
    for name, (base, spread) in spreads.items():
        noise = np.random.default_rng([zlib.crc32(name.encode()), seed]).standard_normal(out[name].shape)
        drawn = base * np.exp(spread * noise) if base else spread * noise
        out[name] = jnp.asarray(drawn.astype(out[name].dtype))
    for name, factor in factors.items():
        out[name] = (out[name] * factor).astype(out[name].dtype)
    return out
```

```python
from contextlib import ExitStack

import concourse.bass as bass
from concourse import mybir

F32 = mybir.dt.float32
BF16 = mybir.dt.bfloat16
ALU = mybir.AluOpType
ACT = mybir.ActivationFunctionType
AX = mybir.AxisListType

P = 128
B, S, D = 4, 1024, 128
H, DH = 16, 8
TB = S // P
T = B * TB
CH = 512
NCH = B * S // CH
HG = 4
NG = H // HG
ROWS = 3 * 3 * DH
MROW = 96
STEPS = (S // CH) * TB
UNITS = HG * TB
LEAD = 4
EPS = 1e-5
E, F = 8, 352
FC = 3
NT = T + E - 1
SHARED_FIRST = 18
ROUTED_BASE = SHARED_FIRST
SHARED_BASE = SHARED_FIRST + NT


def preln_attention_moe_kernel(nc, x_in, w_q, w_k, w_v, w_o, router, w1, w3, w2, ws1, ws3, ws2, out):
    x_tiles = x_in.rearrange("b (t p) d -> p (b t) d", p=P)
    out_tiles = out.rearrange("b (t p) d -> p (b t) d", p=P)
    q_parts = nc.dram_tensor("q_parts", (H, 3 * DH, B * S), BF16, kind="Internal").ap()
    k_parts = nc.dram_tensor("k_parts", (H, 5 * DH, B * S), BF16, kind="Internal").ap()

    x_sorted = nc.dram_tensor("x_sorted", (NT * P, D), F32, kind="Internal").ap()
    y_sorted = nc.dram_tensor("y_sorted", (NT * P, D), F32, kind="Internal").ap()

    with ExitStack() as ctx:
        def sb(name, shape, dt):
            return ctx.enter_context(nc.sbuf_tensor(name, shape, dt))

        def sem(name):
            return ctx.enter_context(nc.semaphore(name))

        x_sb = sb("x_sb", [P, T, D], F32)
        q_aug = sb("q_aug", [P, NG, HG, S], BF16)
        k_aug = sb("k_aug", [P, NG, HG, S], BF16)
        probs = sb("probs", [P, 2, HG, CH], F32)
        xn = sb("xn", [P, T, D], F32)
        attn = sb("attn", [P, T, D], F32)
        xnT = attn[:].rearrange("p t d -> p (t d)")
        v_tok = sb("v_tok", [P, T, D], F32)
        v_aug = sb("v_aug", [P, 2, TB, HG, 32], F32)
        o_rows = sb("o_rows", [P, 2, CH], F32)
        ident = sb("ident", [P, P], F32)
        w_raw = sb("w_raw", [P, 4, P], F32)
        w_T = sb("w_T", [P, 4, P], F32)
        half = HG * CH
        early = probs[:].rearrange("p a h c -> p (a h c)")
        parts = early[:, 0:3 * half // 2].bitcast(BF16).rearrange("p (r a c) -> p r a c", a=3, c=CH)
        resid = early[:, 3 * half // 2:2 * half].rearrange("p (r c) -> p r c", c=CH)
        stats = sb("stats", [P, T, 6], F32)
        mv = sb("mv", [P, T, 2], F32)
        var_eps = sb("var_eps", [P, T], F32)
        std = sb("std", [P, T], F32)
        rstd = sb("rstd", [P, T], F32)
        newton = sb("newton", [P, T], F32)
        neg_max = sb("neg_max", [P, 2, UNITS], F32)
        max_parts = sb("max_parts", [UNITS, 3, P], BF16)
        max_resid = sb("max_resid", [UNITS, P], F32)
        rden = sb("rden", [P, 4, HG], F32)
        attnT = sb("attnT", [P, 2, P], F32)

        w13 = sb("w13", [P, (E + 1) * 2 * F], F32)
        w2_sb = xn[:].rearrange("p t d -> p (t d)")[:, 0:(E + 1) * FC * D]
        router_sb = sb("router_sb", [P, E], F32)
        x2n = v_tok
        x2nT = q_aug[:].rearrange("p a h s -> p (a h s)").bitcast(F32)[:, 0:T * P]
        gated = attn
        gathered = k_aug[:].rearrange("p a h s -> p (a h s)").bitcast(F32)[:, 0:T * P].rearrange(
            "p (t d) -> p t d", d=D)
        ffn = probs[:].rearrange("p a h c -> p (a h c)")

        def piece(start, shape):
            n = 2 * shape
            return ffn[:, start:start + n].rearrange("p (r n) -> p r n", r=2)

        xT_sb = piece(0, P)
        xs_sb = piece(2 * P, P)
        y_sb = piece(4 * P, P)
        silu_sb = piece(6 * P, F)
        g_sb = piece(6 * P + 2 * F, F)
        gT_sb = piece(6 * P + 4 * F, FC * P)
        scratch = k_aug[:].rearrange("p a h s -> p (a h s)").bitcast(F32)[:, T * P:2 * T * P]
        zeros = sb("zeros", [P, P], F32)
        before = sb("before", [P, P], BF16)
        ones = sb("ones", [P, P], BF16)
        expert_no = sb("expert_no", [P, T, E], F32)
        tile_rows = sb("tile_rows", [P, T], F32)
        tile_no = sb("tile_no", [P, NT], F32)
        not_first = sb("not_first", [P, E, T], F32)
        logits = scratch[:, 0 * T * E:1 * T * E].rearrange("p (t e) -> p t e", t=T)
        top = sb("top", [P, T], F32)
        cand = scratch[:, 1 * T * E:2 * T * E].rearrange("p (t e) -> p t e", t=T)
        choice = sb("choice", [P, T], F32)
        onehot = sb("onehot", [P, T, E], BF16)
        cum = scratch[:, 2 * T * E:3 * T * E].rearrange("p (e t) -> p e t", e=E)
        place = scratch[:, 3 * T * E:4 * T * E].rearrange("p (t e) -> p t e", t=T)
        count_cmp = scratch[:, 4 * T * E:5 * T * E].rearrange("p (e t) -> p e t", e=E)
        n_tiles = sb("n_tiles", [P, E], F32)
        last_tile = sb("last_tile", [P, E], F32)
        first_row = sb("first_row", [P, E], F32)
        tile_cmp = sb("tile_cmp", [1, NT, E], F32)
        tile_sum = sb("tile_sum", [1, NT], F32)
        tile_expert = sb("tile_expert", [1, NT], mybir.dt.int32)
        row_f = sb("row_f", [P, T], F32)
        row = sb("row", [P, T], mybir.dt.uint32)
        gate = sb("gate", [P, T], F32)
        gate_e = sb("gate_e", [P, T], F32)

        ps = ctx.enter_context(nc.psum_tensor("ps", [P, 8, CH], F32))
        ST, ACC = 4, 7

        def st_bank(m):
            return ST + m % 3

        def tr_bank(w):
            return 2 * (w % 2)

        x_loaded = [sem(f"x_loaded{i}") for i in range(B)]
        w_loaded = sem("w_loaded")
        ident_zero = sem("ident_zero")
        ident_ready = sem("ident_ready")
        aug_clear = sem("aug_clear")
        vaug_clear = sem("vaug_clear")
        stats_done = sem("stats_done")
        mv_done = sem("mv_done")
        var_done = sem("var_done")
        std_done = sem("std_done")
        rstd_step = sem("rstd_step")
        xn_ready = sem("xn_ready")
        wT_psum = sem("wT_psum")
        wT_ready = sem("wT_ready")
        xT_psum = sem("xT_psum")
        xT_ready = sem("xT_ready")
        qk_psum = sem("qk_psum")
        part1_ready = sem("part1_ready")
        resid_ready = sem("resid_ready")
        part2_ready = sem("part2_ready")
        part3_ready = sem("part3_ready")
        parts_out = [sem(f"parts_out{i}") for i in range(4)]
        v_psum = sem("v_psum")
        v_ready = sem("v_ready")
        aug_loaded = [sem(f"aug_loaded{i}") for i in range(NG)]
        mrow_loaded = [sem(f"mrow_loaded{i}") for i in range(NG)]
        vaug_ready = sem("vaug_ready")
        s_done = sem("s_done")
        max_done = sem("max_done")
        maxT_psum = sem("maxT_psum")
        max_step = sem("max_step")
        st_done = sem("st_done")
        exp_done = sem("exp_done")
        pv_done = sem("pv_done")
        acc_copied = sem("acc_copied")
        o_psum = sem("o_psum")
        rden_ready = sem("rden_ready")
        norm_done = sem("norm_done")
        aT_psum = sem("aT_psum")
        aT_ready = sem("aT_ready")
        proj_psum = sem("proj_psum")
        x2_ready = sem("x2_ready")
        stored = sem("stored")
        ffn_w_loaded = sem("ffn_w_loaded")
        w2_clear = sem("w2_clear")
        consts = sem("consts")
        zero_rows = sem("zero_rows")
        stats2_done = sem("stats2_done")
        mv2_done = sem("mv2_done")
        var2_done = sem("var2_done")
        std2_done = sem("std2_done")
        x2n_ready = sem("x2n_ready")
        x2T_psum = sem("x2T_psum")
        x2T_ready = sem("x2T_ready")
        logits_psum = sem("logits_psum")
        route_step = sem("route_step")
        top_ready = sem("top_ready")
        gate_exp = sem("gate_exp")
        gate_ready = sem("gate_ready")
        onehot_ready = sem("onehot_ready")
        counts_psum = sem("counts_psum")
        table_ready = sem("table_ready")
        rows_ready = sem("rows_ready")
        gated_ready = sem("gated_ready")
        scattered = sem("scattered")
        xs_loaded = [sem(f"xs_loaded{i}") for i in range(2)]
        xsT_psum = sem("xsT_psum")
        ffn_x_ready = sem("ffn_x_ready")
        h_done = sem("h_done")
        silu_done = sem("silu_done")
        g_ready = sem("g_ready")
        gT_psum = sem("gT_psum")
        gT_ready = sem("gT_ready")
        y_psum = sem("y_psum")
        y_read = sem("y_read")
        y_stored = [sem(f"y_stored{i}") for i in range(2)]
        gathered_in = [sem(f"gathered_in{i}") for i in range(4)]
        final_ready = sem("final_ready")

        block = ctx.enter_context(nc.Block())

        def pipeline(eng, n, position):
            for i in range(4):
                position(i, i)
            turns = (n - 1 - 4) // 2
            with eng.Fori(4, 3 + 2 * turns, 2) as i:
                position(i, 4)
                position(i + 1, 5)
            for i in range(4 + 2 * turns, n + 2):
                position(i, i)

        def load_group(sp, row, g):
            heads = slice(g * HG, (g + 1) * HG)
            tok = bass.ds(row * S, S)
            for c in range(3):
                rows = slice(c * 3 * DH, (c + 1) * 3 * DH)
                sp.dma_start(q_aug[rows, g, :, :],
                             q_parts[heads, :, tok].rearrange("h r t -> r h t")).then_inc(aug_loaded[g], 16)
                sp.dma_start(k_aug[rows, g, :, :],
                             k_parts[heads, c * DH:(c + 3) * DH, tok].rearrange("h r t -> r h t")
                             ).then_inc(aug_loaded[g], 16)

        LOADS = 6 * 16
        MROWS = 3 * 16

        def load_max_rows(sp, g):
            for c in range(3):
                dst = q_aug[MROW + c:MROW + c + 1, g, :, :].rearrange("o h (t q) -> o (h t) q", q=P)
                sp.dma_start(dst, max_parts[:, c, :]
                             ).then_inc(mrow_loaded[g], 16)

        def ring_free(eng, signal, base, i, near):
            if near >= 2:
                eng.wait_ge(signal, base + i - 1)
            elif base:
                eng.wait_ge(signal, base)

        def has(i, n):
            return not isinstance(i, int) or i < n

        @block.sync
        def _(sp):
            for b in range(B):
                sp.dma_start(x_sb[:, b * TB:(b + 1) * TB, :],
                             x_tiles[:, b * TB:(b + 1) * TB, :]).then_inc(x_loaded[b], 16)
            for i, w in enumerate((w_q, w_k, w_v, w_o)):
                sp.dma_start(w_raw[:, i, :], w).then_inc(w_loaded, 16)
            for u in range(2 * NCH):
                c, is_k = divmod(u, 2)
                sp.wait_ge(part3_ready, u + 1)
                tok = slice(c * CH, (c + 1) * CH)
                if not is_k:
                    for a in range(3):
                        sp.dma_start(q_parts[:, a * DH:(a + 1) * DH, tok],
                                     parts[:, u % 4, a, :]).then_inc(parts_out[u % 4], 16)
                else:
                    for a in range(5):
                        sp.dma_start(k_parts[:, a * DH:(a + 1) * DH, tok],
                                     parts[:, u % 4, a % 3, :]).then_inc(parts_out[u % 4], 16)
            for i in range(4):
                sp.wait_ge(parts_out[i], 16 * (3, 5)[i % 2] * NCH // 2)
            sp.wait_ge(aug_clear, 3)
            for g in range(3):
                load_group(sp, 0, g)
            sp.wait_ge(max_step, 4)
            load_max_rows(sp, 0)
            sp.dma_start(router_sb[:], router).then_inc(ffn_w_loaded, 16)
            w13_v = w13[:].rearrange("p (e k f) -> p e k f", k=2, f=F)
            sp.dma_start(w13_v[:, 0:E, 0, :], w1.rearrange("e d f -> d e f")).then_inc(ffn_w_loaded, 16)
            sp.dma_start(w13_v[:, 0:E, 1, :], w3.rearrange("e d f -> d e f")).then_inc(ffn_w_loaded, 16)
            sp.dma_start(w13_v[:, E, 0, :], ws1).then_inc(ffn_w_loaded, 16)
            sp.dma_start(w13_v[:, E, 1, :], ws3).then_inc(ffn_w_loaded, 16)
            sp.wait_ge(w2_clear, 1)
            w2_v = w2_sb.rearrange("p (e c d) -> p e c d", c=FC, d=D)
            for c in range(FC - 1):
                sp.dma_start(w2_v[:, 0:E, c, :], w2[:, c * P:(c + 1) * P, :].rearrange("e f d -> f e d")
                             ).then_inc(ffn_w_loaded, 16)
                sp.dma_start(w2_v[:, E, c, :], ws2[c * P:(c + 1) * P, :]).then_inc(ffn_w_loaded, 16)
            tail = FC * P - F
            sp.dma_start(w2_v[tail:P, 0:E, FC - 1, :], w2[:, (FC - 1) * P:F, :].rearrange("e f d -> f e d")
                         ).then_inc(ffn_w_loaded, 16)
            sp.dma_start(w2_v[tail:P, E, FC - 1, :], ws2[(FC - 1) * P:F, :]).then_inc(ffn_w_loaded, 16)
            for j in range(NT):
                sp.dma_start(x_sorted[j * P:(j + 1) * P, :], zeros[:]).then_inc(zero_rows, 16)

            def batch_row(b, last):
                for g in range(NG):
                    if not (last and g > 0):
                        if g > 0:
                            sp.wait_ge(st_done, (b * NG + g) * HG * STEPS)
                            load_group(sp, b + 1, g - 1)
                        else:
                            sp.wait_ge(st_done, b * NG * HG * STEPS + 1)
                            load_group(sp, b, 3)
                    if not (last and g == NG - 1):
                        sp.wait_ge(max_step, (b * NG + g + 2) * 4)
                        load_max_rows(sp, (g + 1) % NG)

            with sp.Fori(0, B - 1) as b:
                batch_row(b, False)
            batch_row(B - 1, True)

            sp.wait_ge(scattered, 16 * T)

            def load_sorted(i, near, par):
                sp.dma_start(xs_sb[:, par, :], x_sorted[bass.ds(i * P, P), :]).then_inc(xs_loaded[par], 16)

            for i in range(2):
                sp.dma_start(xs_sb[:, i, :], x_sorted[i * P:(i + 1) * P, :]).then_inc(xs_loaded[i], 16)
            turns = (NT - 2) // 2
            with sp.Fori(2, 1 + 2 * turns, 2) as i:
                for p in range(2):
                    sp.wait_ge(xsT_psum, i + p - 1)
                    sp.dma_start(xs_sb[:, p, :], x_sorted[bass.ds((i + p) * P, P), :]).then_inc(xs_loaded[p], 16)
            for i in range(2 + 2 * turns, NT):
                sp.wait_ge(xsT_psum, i - 1)
                sp.dma_start(xs_sb[:, i % 2, :], x_sorted[i * P:(i + 1) * P, :]).then_inc(xs_loaded[i % 2], 16)
            for q in range(4):
                sp.wait_ge(final_ready, q + 1)
                sp.dma_start(out_tiles[:, 8 * q:8 * q + 8, :], x_sb[:, 8 * q:8 * q + 8, :]).then_inc(stored, 16)
            sp.wait_ge(stored, 16 * 4)

        @block.gpsimd
        def _(pool):
            pool.memset(ident[:], 0.0).then_inc(ident_zero, 1)
            pool.wait_ge(ident_zero, 1)
            pool.affine_select(out=ident[:], in_=ident[:], compare_op=ALU.not_equal, fill=1.0, base=0,
                               pattern=[[-1, P]], channel_multiplier=1).then_inc(ident_ready, 1)
            pool.wait_ge(ident_ready, 1)
            pool.memset(q_aug[64:P, :, :, :], 0.0).then_inc(aug_clear, 1)
            pool.wait_ge(aug_clear, 1)
            pool.memset(k_aug[64:P, :, :, :], 0.0).then_inc(aug_clear, 1)
            pool.wait_ge(aug_clear, 2)
            pool.memset(k_aug[MROW:MROW + 3, :, :, :], 1.0).then_inc(aug_clear, 1)
            pool.wait_ge(aug_clear, 3)
            pool.memset(v_aug[:], 0.0).then_inc(vaug_clear, 1)
            pool.wait_ge(vaug_clear, 1)
            pool.memset(v_aug[:, :, :, :, DH:DH + 1], 1.0).then_inc(vaug_clear, 1)
            pool.wait_ge(vaug_clear, 2)
            n_consts = 0

            def made(ins):
                nonlocal n_consts
                n_consts += 1
                ins.then_inc(consts, 1)
                pool.wait_ge(consts, n_consts)

            made(pool.memset(zeros[:], 0.0))
            made(pool.memset(ones[:], 1.0))
            made(pool.affine_select(out=before[:], in_=ones[:], compare_op=ALU.is_gt, fill=0.0, base=0,
                                    pattern=[[1, P]], channel_multiplier=-1))
            for t, pattern in ((expert_no, [[0, T], [1, E]]), (tile_rows, [[P, T]]), (tile_no, [[1, NT]])):
                made(pool.iota(t[:], pattern, base=0, channel_multiplier=0, allow_small_or_imprecise_dtypes=True))
            made(pool.memset(not_first[:], 1.0))
            made(pool.memset(not_first[:, :, 0:1], 0.0))
            pool.wait_ge(v_ready, NCH)
            pool.wait_ge(xT_psum, NCH)
            pool.memset(w2_sb.rearrange("p (e c d) -> p e c d", c=FC, d=D)[0:FC * P - F, :, FC - 1, :], 0.0
                        ).then_inc(w2_clear, 1)
            pool.wait_ge(w2_clear, 1)

            def copy_v(row, g, slot):
                for j in range(HG):
                    c = (g * HG + j) * DH
                    pool.tensor_copy(v_aug[:, slot, :, j, 0:DH],
                                     v_tok[:, bass.ds(row * TB, TB), c:c + DH]).then_inc(vaug_ready, 1)

            copy_v(0, 0, 0)

            def batch_row(b, last):
                for g in range(NG):
                    if last and g == NG - 1:
                        continue
                    if g > 0:
                        pool.wait_ge(pv_done, (b * NG + g) * STEPS)
                    else:
                        pool.wait_ge(pv_done, b * NG * STEPS + 1)
                    copy_v(b + (g + 1) // NG, (g + 1) % NG, (g + 1) % 2)

            with pool.Fori(0, B - 1) as b:
                batch_row(b, False)
            batch_row(B - 1, True)

            pool.wait_ge(zero_rows, 16 * NT)
            pool.wait_ge(rows_ready, 1)
            pool.wait_ge(gated_ready, 1)
            for t in range(T):
                pool.indirect_dma_start(out=x_sorted, out_offset=bass.IndirectOffsetOnAxis(ap=row[:, t:t + 1], axis=0),
                                        in_=gated[:, t, :], in_offset=None).then_inc(scattered, 16)
            pool.wait_ge(y_stored[0], 16 * ((NT + 1) // 2))
            pool.wait_ge(y_stored[1], 16 * (NT // 2))
            for t in range(T):
                pool.indirect_dma_start(out=gathered[:, t, :], out_offset=None, in_=y_sorted,
                                        in_offset=bass.IndirectOffsetOnAxis(ap=row[:, t:t + 1], axis=0)
                                        ).then_inc(gathered_in[t // 8], 16)

        @block.scalar
        def _(act):
            act.wait_ge(var_done, 1)
            act.activation(std[:], var_eps[:], ACT.Sqrt).then_inc(std_done, 1)
            act.wait_ge(wT_psum, 1)
            act.activation(w_T[:, 0, :], ps[:, 7, 0:P], ACT.Copy, scale=float(DH) ** -0.5).then_inc(wT_ready, 1)
            act.activation(w_T[:, 1:4, :], ps[:, 7, P:4 * P].rearrange("p (w e) -> p w e", e=P),
                           ACT.Copy).then_inc(wT_ready, 1)
            for c in range(NCH):
                for k in range(2):
                    u = 2 * c + k
                    act.wait_ge(qk_psum, u + 1)
                    if u >= 4:
                        act.wait_ge(parts_out[u % 4], 16 * (3, 5)[k] * (u // 4))
                    act.activation(parts[:, u % 4, 0, :], ps[:, 2 + u % 2, :], ACT.Copy).then_inc(part1_ready, 1)
                    act.wait_ge(resid_ready, u + 1)
                    act.activation(parts[:, u % 4, 1, :], resid[:, u % 2, :], ACT.Copy).then_inc(part2_ready, 1)
                act.wait_ge(v_psum, c + 1)
                act.activation(v_tok[:, 4 * c:4 * c + 4, :],
                               ps[:, 4 + c % 2, :].rearrange("p (t e) -> p t e", e=P), ACT.Copy).then_inc(v_ready, 1)

            def batch_row(b, last):
                for n in range(NG * STEPS):
                    for j in range(HG):
                        act.wait_ge(st_done, (b * NG * STEPS + n) * HG + j + 1)
                        if n >= 2 and j == 0:
                            act.wait_ge(pv_done, b * NG * STEPS + n - 1)
                        act.activation(probs[:, n % 2, j, :], ps[:, st_bank(n % STEPS * HG + j), :],
                                       ACT.Exp).then_inc(exp_done, 1)
                    if n % TB == 0 and n > 0:
                        copy_acc(b, n // TB - 1)
                copy_acc(b, NG * STEPS // TB - 1)

            def copy_acc(b, half):
                halves = NG * STEPS // TB
                act.wait_ge(pv_done, b * NG * STEPS + (half + 1) * TB)
                if half >= 2:
                    act.wait_ge(o_psum, b * halves + half - 1)
                act.activation(o_rows[:, half % 2, :], ps[:, ACC, :], ACT.Copy).then_inc(acc_copied, 1)

            with act.Fori(0, B - 1) as b:
                batch_row(b, False)
            batch_row(B - 1, True)

            for t in range(T):
                act.wait_ge(aT_psum, t + 1)
                if t >= 2:
                    act.wait_ge(proj_psum, t - 1)
                act.activation(attnT[:, t % 2, :], ps[:, t % 2, 0:P], ACT.Copy).then_inc(aT_ready, 1)

            act.wait_ge(var2_done, 1)
            act.activation(std[:], var_eps[:], ACT.Sqrt).then_inc(std2_done, 1)
            for c in range(NCH):
                act.wait_ge(x2T_psum, c + 1)
                act.activation(x2nT[:, c * CH:(c + 1) * CH], ps[:, c % 2, :], ACT.Copy).then_inc(x2T_ready, 1)
            act.wait_ge(top_ready, 1)
            act.activation(gate_e[:], top[:], ACT.Exp, scale=-1.0).then_inc(gate_exp, 1)

            def silu(base, i, near):
                act.wait_ge(h_done, base + i + 1)
                ring_free(act, g_ready, base, i, near)
                act.activation(silu_sb[:, near % 2, :], ps[:, near % 2, 0:F], ACT.Silu).then_inc(silu_done, 1)

            def place_shared(base, tile, i, near):
                ring_free(act, h_done, base, i, near)
                act.activation(xT_sb[:, near % 2, :], x2nT[:, bass.ds((tile + i) * P, P)], ACT.Copy
                               ).then_inc(ffn_x_ready, 1)

            def place_routed(i, near):
                act.wait_ge(xsT_psum, i + 1)
                ring_free(act, h_done, ROUTED_BASE, i, near)
                act.activation(xT_sb[:, near % 2, :], ps[:, 4, 0:P], ACT.Copy).then_inc(ffn_x_ready, 1)

            def shared_run(base, tile, n):
                def position(i, near):
                    if near == 0:
                        place_shared(base, tile, 0, 0)
                    if has(i + 1, n):
                        place_shared(base, tile, i + 1, near + 1)
                    if has(i, n):
                        silu(base, i, near)
                return position

            def routed(i, near):
                if near == 0:
                    place_routed(0, 0)
                if has(i + 1, NT):
                    place_routed(i + 1, near + 1)
                if has(i, NT):
                    silu(ROUTED_BASE, i, near)
                if near >= 2:
                    p = near % 2
                    act.wait_ge(y_psum, ROUTED_BASE + i - 1)
                    if near >= 4:
                        act.wait_ge(y_stored[p], (i - p - 2) * 8)
                    act.activation(y_sb[:, p, :], ps[:, 7, 0:P], ACT.Copy).then_inc(y_read, 1)
                    act.wait_ge(y_read, ROUTED_BASE + i - 1)
                    act.dma_start(y_sorted[bass.ds((i - 2) * P, P), :], y_sb[:, p, :]).then_inc(y_stored[p], 16)

            pipeline(act, SHARED_FIRST, shared_run(0, 0, SHARED_FIRST))
            pipeline(act, NT, routed)
            pipeline(act, T - SHARED_FIRST, shared_run(SHARED_BASE, SHARED_FIRST, T - SHARED_FIRST))

        @block.tensor
        def _(pe):
            pe.wait_ge(ident_ready, 1)
            pe.wait_ge(w_loaded, 64)
            for i in range(4):
                mm = pe.transpose(ps[:, 7, i * P:(i + 1) * P], w_raw[:, i, :], ident[:])
            mm.then_inc(wT_psum, 1)
            for c in range(NCH):
                pe.wait_ge(xn_ready, 4 * c + 4)
                if c >= 2:
                    pe.wait_ge(xT_ready, c - 1)
                for i in range(4):
                    mm = pe.transpose(ps[:, c % 2, i * P:(i + 1) * P], xn[:, 4 * c + i, :], ident[:])
                mm.then_inc(xT_psum, 1)
                if c == 0:
                    pe.wait_ge(wT_ready, 2)
                pe.wait_ge(xT_ready, c + 1)
                for k in range(2):
                    u = 2 * c + k
                    if u >= 2:
                        pe.wait_ge(resid_ready, u - 1)
                    pe.matmul(ps[:, 2 + u % 2, :], w_T[:, k, :], xnT[:, c * CH:(c + 1) * CH],
                              start=True, stop=True).then_inc(qk_psum, 1)
                if c >= 2:
                    pe.wait_ge(v_ready, c - 1)
                for i in range(4):
                    t = 4 * c + i
                    mm = pe.matmul(ps[:, 4 + c % 2, i * P:(i + 1) * P], xnT[:, t * P:(t + 1) * P], w_T[:, 2, :],
                                   start=True, stop=True)
                mm.then_inc(v_psum, 1)

            def score_unit(row, w):
                g, u = divmod(w, UNITS)
                j, t = divmod(u, TB)
                if u == 0:
                    pe.wait_ge(aug_loaded[g % NG], (row + g // NG + 1) * LOADS)
                for half in range(2):
                    mm = pe.matmul(ps[:, tr_bank(w) + half, :], q_aug[0:MROW, g % NG, j, t * P:(t + 1) * P],
                                   k_aug[0:MROW, g % NG, j, half * CH:(half + 1) * CH], start=True, stop=True)
                mm.then_inc(s_done, 1)

            def scores_T(n, j):
                g, s = divmod(n, STEPS)
                half, t = divmod(s, TB)
                pe.matmul(ps[:, st_bank(s * HG + j), :], k_aug[:, g % NG, j, t * P:(t + 1) * P],
                          q_aug[:, g % NG, j, half * CH:(half + 1) * CH], start=True, stop=True
                          ).then_inc(st_done, 1)

            def max_transpose(group, parity, w):
                pe.wait_ge(max_done, (group + 1) * UNITS)
                pe.transpose(ps[0:UNITS, tr_bank(w), 0:P], neg_max[:, parity, :], ident[:]).then_inc(maxT_psum, 1)

            def out_transpose(b, half, w):
                pe.wait_ge(acc_copied, b * 2 * NG + half + 1)
                for i in range(4):
                    mm = pe.transpose(ps[:, tr_bank(w), i * P:(i + 1) * P], o_rows[:, half % 2, i * P:(i + 1) * P],
                                      ident[:])
                mm.then_inc(o_psum, 1)

            pe.wait_ge(part3_ready, 2 * NCH)
            pe.wait_ge(v_ready, NCH)
            for w in range(UNITS + 2 * LEAD):
                if w >= 2:
                    pe.wait_ge(max_done, w - 1)
                score_unit(0, w)
            pe.wait_ge(max_done, UNITS + 2 * LEAD - 1)
            max_transpose(0, 0, UNITS + 2 * LEAD)
            pe.wait_ge(mrow_loaded[0], MROWS)
            for j in range(HG):
                if j == 3:
                    pe.wait_ge(exp_done, 1)
                scores_T(0, j)

            def values(b, n):
                g, s = divmod(n, STEPS)
                half, t = divmod(s, TB)
                if s == 0:
                    pe.wait_ge(vaug_ready, (b * NG + g + 1) * HG)
                if t == 0 and n > 0:
                    pe.wait_ge(acc_copied, b * 2 * NG + n // TB)
                pe.wait_ge(exp_done, (b * NG * STEPS + n + 1) * HG)
                for j in range(HG):
                    mm = pe.matmul(ps[32 * j:32 * j + 32, ACC, :], v_aug[:, g % 2, t, j, :],
                                   probs[:, n % 2, j, :], start=(t == 0), stop=(t == TB - 1),
                                   tile_position=(0, 32 * j))
                mm.then_inc(pv_done, 1)

            def batch_row(b, last):
                per_row = NG * STEPS
                for n in range(per_row):
                    g, s = divmod(n, STEPS)
                    if n == per_row - 1:
                        values(b, n)
                    for pair in range(2):
                        for j in (2 * pair, 2 * pair + 1):
                            if last and n == per_row - 1:
                                continue
                            m = (n + 1) % STEPS * HG + j
                            if m == 0:
                                pe.wait_ge(mrow_loaded[(g + 1) % NG], (b + (g + 1) // NG + 1) * MROWS)
                            used = {0: 1, 1: 4, 2: 4}.get(m, 3)
                            pe.wait_ge(exp_done, (b * per_row + n + 1) * HG + j - used + 1)
                            scores_T(n + 1, j)
                        w = UNITS + 2 * LEAD + 2 * n + pair
                        if not (last and w >= NG * UNITS):
                            pe.wait_ge(max_done, b * NG * UNITS + w - 1)
                            if pair == 0 and s in (2, TB + 2) and n > 2:
                                pe.wait_ge(norm_done, b * 2 * NG + n // TB)
                            if pair == 0 and n == 0:
                                pe.wait_ge(max_step, 4)
                            if pair == 0 and s == STEPS - LEAD + 1:
                                pe.wait_ge(max_step, (b * NG + g + 2) * 4)
                            score_unit(b, w)
                    if n < per_row - 1:
                        values(b, n)
                    w = UNITS + 2 * LEAD + 2 * (n + 1)
                    if s % TB == 1 and n > 1 or s == STEPS - LEAD and not (last and g == NG - 1):
                        pe.wait_ge(max_done, b * NG * UNITS + min(w - 1, NG * UNITS if last else w))
                        if last and g == NG - 1:
                            pe.wait_ge(norm_done, b * 2 * NG + n // TB - 1)
                    if s == STEPS - LEAD and not (last and g == NG - 1):
                        max_transpose(b * NG + g + 1, (g + 1) % 2, w)
                    if s % TB == 1 and n > 1:
                        out_transpose(b, n // TB - 1, w)
                pe.wait_ge(max_done, b * NG * UNITS + min(w - 1, NG * UNITS if last else w))
                if last:
                    pe.wait_ge(norm_done, b * 2 * NG + 2 * NG - 1)
                out_transpose(b, 2 * NG - 1, w)
                if not last:
                    pe.wait_ge(norm_done, b * 2 * NG + 2 * NG)
                pe.wait_ge(acc_copied, b * 2 * NG + 2 * NG)

            with pe.Fori(0, B - 1) as b:
                batch_row(b, False)
            batch_row(B - 1, True)

            for t in range(T):
                if t == 0:
                    pe.wait_ge(norm_done, B * 2 * NG)
                if t >= 2:
                    pe.wait_ge(aT_ready, t - 1)
                pe.transpose(ps[:, t % 2, 0:P], attn[:, t, :], ident[:]).then_inc(aT_psum, 1)
                pe.wait_ge(aT_ready, t + 1)
                if t >= 2:
                    pe.wait_ge(x2_ready, t - 1)
                pe.matmul(ps[:, 2 + t % 2, 0:P], attnT[:, t % 2, :], w_T[:, 3, :],
                          start=True, stop=True).then_inc(proj_psum, 1)

            for c in range(NCH):
                pe.wait_ge(x2n_ready, 4 * c + 4)
                if c >= 2:
                    pe.wait_ge(x2T_ready, c - 1)
                for i in range(4):
                    mm = pe.transpose(ps[:, c % 2, i * P:(i + 1) * P], x2n[:, 4 * c + i, :], ident[:])
                mm.then_inc(x2T_psum, 1)
                pe.wait_ge(x2T_ready, c + 1)
                if c == 0:
                    pe.wait_ge(ffn_w_loaded, 16 * 11)
                for i in range(4):
                    t = 4 * c + i
                    mm = pe.matmul(ps[:, 4, t * E:(t + 1) * E], x2nT[:, t * P:(t + 1) * P], router_sb[:],
                                   start=True, stop=True)
            mm.then_inc(logits_psum, 1)
            pe.wait_ge(onehot_ready, 1)
            flat = onehot[:].rearrange("p t e -> p (t e)")
            pe.matmul(ps[:, 5, 0:T * E], before[:], flat, start=True, stop=True)
            pe.matmul(ps[:, 6, 0:T * E], ones[:], flat, start=True, stop=True).then_inc(counts_psum, 1)
            pe.wait_ge(rows_ready, 1)

            def hidden(base, i, near, expert):
                p = near % 2
                pe.wait_ge(ffn_x_ready, base + i + 1)
                ring_free(pe, g_ready, base, i, near)
                for k in range(2):
                    mm = pe.matmul(ps[:, 2 * k + p, 0:F], xT_sb[:, p, :], w13[:, bass.ds(expert * 2 * F + k * F, F)],
                                   start=True, stop=True)
                mm.then_inc(h_done, 1)

            def turn_g(base, i, near):
                p = near % 2
                pe.wait_ge(g_ready, base + i + 1)
                ring_free(pe, gT_ready, base, i, near)
                for c in range(FC):
                    f = min(c * P, F - P)
                    mm = pe.transpose(ps[:, 5 + p, c * P:(c + 1) * P], g_sb[:, p, f:f + P], ident[:])
                mm.then_inc(gT_psum, 1)

            def outputs(base, i, near, expert):
                pe.wait_ge(gT_ready, base + i + 1)
                if base or near >= 1:
                    pe.wait_ge(y_read, base + i)
                for c in range(FC):
                    mm = pe.matmul(ps[:, 7, 0:D], gT_sb[:, near % 2, c * P:(c + 1) * P],
                                   w2_sb[:, bass.ds((expert * FC + c) * D, D)], start=(c == 0), stop=(c == FC - 1))
                mm.then_inc(y_psum, 1)

            def shared_run(base, n):
                def position(i, near):
                    if has(i, n):
                        hidden(base, i, near, E)
                    if near >= 1 and has(i - 1, n):
                        turn_g(base, i - 1, near - 1)
                    if near >= 2:
                        outputs(base, i - 2, near - 2, E)
                return position

            def turn_x(i, near):
                pe.wait_ge(xs_loaded[near % 2], x_loads(i, near))
                if near >= 1:
                    pe.wait_ge(ffn_x_ready, ROUTED_BASE + i)
                pe.transpose(ps[:, 4, 0:P], xs_sb[:, near % 2, :], ident[:]).then_inc(xsT_psum, 1)

            def x_loads(i, near):
                return (i - near % 2) * 8 + 16

            def expert_of(i):
                return pe.value_load(tile_expert[0:1, bass.ds(i, 1)], min_val=0, max_val=E - 1)

            def routed(i, near):
                if near == 0:
                    turn_x(0, 0)
                if has(i + 1, NT):
                    turn_x(i + 1, near + 1)
                if has(i, NT):
                    hidden(ROUTED_BASE, i, near, expert_of(i))
                if near >= 1 and has(i - 1, NT):
                    turn_g(ROUTED_BASE, i - 1, near - 1)
                if near >= 2:
                    outputs(ROUTED_BASE, i - 2, near - 2, expert_of(i - 2))

            pipeline(pe, SHARED_FIRST, shared_run(0, SHARED_FIRST))
            pe.wait_ge(table_ready, 1)
            pipeline(pe, NT, routed)
            pipeline(pe, T - SHARED_FIRST, shared_run(SHARED_BASE, T - SHARED_FIRST))

        @block.vector
        def _(dve):
            for t in range(T):
                if t % TB == 0:
                    dve.wait_ge(x_loaded[t // TB], 16)
                dve.bn_stats(stats[:, t, :], x_sb[:, t, :]).then_inc(stats_done, 1)
            for t in range(T):
                dve.wait_ge(stats_done, t + 1)
                dve.bn_aggr(mv[:, t, :], stats[:, t, :]).then_inc(mv_done, 1)
            dve.wait_ge(mv_done, T)
            dve.tensor_scalar(var_eps[:], mv[:, :, 1], EPS, None, ALU.add).then_inc(var_done, 1)
            dve.wait_ge(std_done, 1)
            dve.reciprocal(rstd[:], std[:]).then_inc(rstd_step, 1)

            def refine(base):
                dve.wait_ge(rstd_step, base + 1)
                dve.tensor_tensor(newton[:], rstd[:], rstd[:], ALU.mult).then_inc(rstd_step, 1)
                dve.wait_ge(rstd_step, base + 2)
                dve.tensor_tensor(newton[:], newton[:], var_eps[:], ALU.mult).then_inc(rstd_step, 1)
                dve.wait_ge(rstd_step, base + 3)
                dve.tensor_scalar(newton[:], newton[:], -0.5, 1.5, ALU.mult, ALU.add).then_inc(rstd_step, 1)
                dve.wait_ge(rstd_step, base + 4)
                dve.tensor_tensor(rstd[:], rstd[:], newton[:], ALU.mult).then_inc(rstd_step, 1)
                dve.wait_ge(rstd_step, base + 5)

            refine(0)

            def normalise(t):
                dve.tensor_scalar(xn[:, t, :], x_sb[:, t, :], mv[:, t, 0:1], rstd[:, t:t + 1],
                                  ALU.subtract, ALU.mult).then_inc(xn_ready, 1)

            for t in range(4):
                normalise(t)
            for c in range(NCH):
                dve.wait_ge(xT_psum, c + 1)
                dve.tensor_copy(xnT[:, c * CH:(c + 1) * CH], ps[:, c % 2, :]).then_inc(xT_ready, 1)
                if c + 1 < NCH:
                    for t in range(4 * c + 4, 4 * c + 8):
                        normalise(t)
                for k in range(2):
                    u = 2 * c + k
                    dve.wait_ge(part1_ready, u + 1)
                    dve.tensor_tensor(resid[:, u % 2, :], ps[:, 2 + u % 2, :], parts[:, u % 4, 0, :],
                                      ALU.subtract).then_inc(resid_ready, 1)
                for k in range(2):
                    u = 2 * c + k
                    dve.wait_ge(part2_ready, u + 1)
                    dve.tensor_tensor(parts[:, u % 4, 2, :], resid[:, u % 2, :], parts[:, u % 4, 1, :],
                                      ALU.subtract).then_inc(part3_ready, 1)

            def row_max(base, w):
                dve.wait_ge(s_done, base + w + 1)
                u = w % UNITS
                dve.tensor_reduce(neg_max[:, w // UNITS % 2, u:u + 1], ps[:, tr_bank(w):tr_bank(w) + 2, :],
                                  mybir.AxisListType.XY, ALU.max, negate=True).then_inc(max_done, 1)

            def split_max(group, slot_free, w):
                dve.wait_ge(maxT_psum, group + 1)
                if slot_free is not None:
                    dve.wait_ge(*slot_free)
                src = ps[0:UNITS, tr_bank(w), 0:P]
                dve.tensor_copy(max_parts[:, 0, :], src).then_inc(max_step, 1)
                dve.wait_ge(max_step, group * 4 + 1)
                dve.tensor_tensor(max_resid[:], src, max_parts[:, 0, :], ALU.subtract).then_inc(max_step, 1)
                dve.wait_ge(max_step, group * 4 + 2)
                dve.tensor_copy(max_parts[:, 1, :], max_resid[:]).then_inc(max_step, 1)
                dve.wait_ge(max_step, group * 4 + 3)
                dve.tensor_tensor(max_parts[:, 2, :], max_resid[:], max_parts[:, 1, :],
                                  ALU.subtract).then_inc(max_step, 1)

            for w in range(UNITS + 2 * LEAD):
                row_max(0, w)
            split_max(0, None, UNITS + 2 * LEAD)

            def norm(b, half, w):
                g, q = divmod(half, 2)
                dve.wait_ge(o_psum, b * 2 * NG + half + 1)
                src = ps[:, tr_bank(w), :].rearrange("p (t h r) -> p t h r", t=4, h=HG)
                dve.reciprocal(rden[:], src[:, :, :, DH]).then_inc(rden_ready, 1)
                dve.wait_ge(rden_ready, b * 2 * NG + half + 1)
                dst = attn[:, bass.ds(b * TB + 4 * q, 4), g * HG * DH:(g + 1) * HG * DH]
                dve.tensor_tensor(dst.rearrange("p t (h d) -> p t h d", d=DH), src[:, :, :, 0:DH],
                                  rden[:].rearrange("p t (h o) -> p t h o", o=1).broadcast_to([P, 4, HG, DH]),
                                  ALU.mult).then_inc(norm_done, 1)

            def batch_row(b, last):
                for n in range(NG * STEPS):
                    g, s = divmod(n, STEPS)
                    w = UNITS + 2 * LEAD + 2 * n
                    if s == STEPS - LEAD + 1 and not (last and g == NG - 1):
                        split_max(b * NG + g + 1, (mrow_loaded[g], (b + 1) * MROWS), w)
                    if n % TB == 2 and n > 2:
                        norm(b, n // TB - 1, w)
                    for v in (w, w + 1):
                        if not (last and v >= NG * UNITS):
                            row_max(b * NG * UNITS, v)
                norm(b, 2 * NG - 1, w + 2)

            with dve.Fori(0, B - 1) as b:
                batch_row(b, False)
            batch_row(B - 1, True)

            for t in range(T):
                dve.wait_ge(proj_psum, t + 1)
                dve.tensor_tensor(x_sb[:, t, :], ps[:, 2 + t % 2, 0:P], x_sb[:, t, :], ALU.add).then_inc(x2_ready, 1)
                dve.wait_ge(x2_ready, t + 1)
                dve.bn_stats(stats[:, t, :], x_sb[:, t, :]).then_inc(stats2_done, 1)
            for t in range(T):
                dve.wait_ge(stats2_done, t + 1)
                dve.bn_aggr(mv[:, t, :], stats[:, t, :]).then_inc(mv2_done, 1)
            dve.wait_ge(mv2_done, T)
            dve.tensor_scalar(var_eps[:], mv[:, :, 1], EPS, None, ALU.add).then_inc(var2_done, 1)
            dve.wait_ge(std2_done, 1)
            dve.reciprocal(rstd[:], std[:]).then_inc(rstd_step, 1)
            refine(5)
            for t in range(T):
                dve.tensor_scalar(x2n[:, t, :], x_sb[:, t, :], mv[:, t, 0:1], rstd[:, t:t + 1],
                                  ALU.subtract, ALU.mult).then_inc(x2n_ready, 1)

            def over_experts(a):
                return a.rearrange("p (t o) -> p t o", o=1).broadcast_to([P, T, E])

            def over_tokens(a):
                return a.rearrange("p (o e) -> p o e", o=1).broadcast_to([P, T, E])

            n_steps = 0

            def step(ins):
                nonlocal n_steps
                n_steps += 1
                ins.then_inc(route_step, 1)
                dve.wait_ge(route_step, n_steps)

            dve.wait_ge(consts, 8)
            dve.wait_ge(logits_psum, 1)
            step(dve.tensor_copy(logits.rearrange("p t e -> p (t e)"), ps[:, 4, 0:T * E]))
            dve.tensor_reduce(top[:], logits, AX.X, ALU.max).then_inc(top_ready, 1)
            dve.wait_ge(top_ready, 1)
            step(dve.tensor_tensor(cand, logits, over_experts(top[:]), ALU.not_equal))
            step(dve.scalar_tensor_tensor(out=cand, in0=cand, scalar=float(2 * E), in1=expert_no[:],
                                          op0=ALU.mult, op1=ALU.add))
            step(dve.tensor_reduce(choice[:], cand, AX.X, ALU.min))
            dve.tensor_tensor(onehot[:], cand, over_experts(choice[:]), ALU.is_equal).then_inc(onehot_ready, 1)
            dve.wait_ge(gate_exp, 1)
            step(dve.tensor_scalar(gate_e[:], gate_e[:], 1.0, None, ALU.add))
            step(dve.reciprocal(gate[:], gate_e[:]))
            dve.tensor_tensor(gated[:], x2n[:], gate[:].rearrange("p (t o) -> p t o", o=1).broadcast_to([P, T, D]),
                              ALU.mult).then_inc(gated_ready, 1)
            dve.wait_ge(counts_psum, 1)
            per_tile = ps[:, 6, 0:T * E].rearrange("p (t e) -> p t e", e=E)
            step(dve.tensor_copy(cum, per_tile.rearrange("p t e -> p e t")))
            step(dve.tensor_tensor_scan(cum.rearrange("p e t -> p (e t)"), not_first[:].rearrange("p e t -> p (e t)"),
                                        cum.rearrange("p e t -> p (e t)"), 0.0, ALU.mult, ALU.add))
            step(dve.tensor_tensor(count_cmp, cum[:, :, T - 1:T].broadcast_to([P, E, T]),
                                   tile_rows[:].rearrange("p (o t) -> p o t", o=1).broadcast_to([P, E, T]), ALU.is_gt))
            step(dve.tensor_reduce(n_tiles[:], count_cmp, AX.X, ALU.add))
            step(dve.tensor_tensor_scan(last_tile[:], ones[:, 0:E], n_tiles[:], 0.0, ALU.mult, ALU.add))
            step(dve.tensor_tensor(first_row[:], last_tile[:], n_tiles[:], ALU.subtract))
            step(dve.tensor_scalar(first_row[:], first_row[:], float(P), None, ALU.mult))
            step(dve.tensor_tensor(place, per_tile, cum.rearrange("p e t -> p t e"), ALU.subtract))
            step(dve.scalar_tensor_tensor(out=place, in0=place, scalar=-1.0,
                                          in1=ps[:, 5, 0:T * E].rearrange("p (t e) -> p t e", e=E),
                                          op0=ALU.mult, op1=ALU.add))
            step(dve.tensor_tensor(place, place, over_tokens(first_row[:]), ALU.add))
            step(dve.tensor_tensor(place, place, onehot[:], ALU.mult))
            step(dve.tensor_reduce(row_f[:], place, AX.X, ALU.add))
            dve.tensor_copy(row[:], row_f[:]).then_inc(rows_ready, 1)
            step(dve.tensor_tensor(tile_cmp[:], tile_no[0:1, :].rearrange("p (j o) -> p j o", o=1).broadcast_to([1, NT, E]),
                                   last_tile[0:1, :].rearrange("p (o e) -> p o e", o=1).broadcast_to([1, NT, E]),
                                   ALU.is_ge))
            step(dve.tensor_reduce(tile_sum[:], tile_cmp[:], AX.X, ALU.add))
            dve.tensor_scalar(tile_expert[:], tile_sum[:], float(E - 1), None, ALU.min).then_inc(table_ready, 1)

            def gate_hidden(base, i, near):
                p = near % 2
                dve.wait_ge(silu_done, base + i + 1)
                ring_free(dve, gT_psum, base, i, near)
                dve.tensor_tensor(g_sb[:, p, :], silu_sb[:, p, :], ps[:, 2 + p, 0:F], ALU.mult).then_inc(g_ready, 1)

            def keep_gT(base, i, near):
                p = near % 2
                dve.wait_ge(gT_psum, base + i + 1)
                ring_free(dve, y_psum, base, i, near)
                dve.tensor_copy(gT_sb[:, p, :], ps[:, 5 + p, 0:FC * P]).then_inc(gT_ready, 1)

            def shared_run(base, tile, n):
                def position(i, near):
                    if has(i, n):
                        gate_hidden(base, i, near)
                    if near >= 1 and has(i - 1, n):
                        keep_gT(base, i - 1, near - 1)
                    if near >= 2:
                        dve.wait_ge(y_psum, base + i - 1)
                        x_t = x_sb[:, bass.ds(tile + i - 2, 1), :].rearrange("p o d -> p (o d)")
                        dve.tensor_tensor(x_t, ps[:, 7, 0:D], x_t, ALU.add).then_inc(y_read, 1)
                return position

            def routed(i, near):
                if has(i, NT):
                    gate_hidden(ROUTED_BASE, i, near)
                if near >= 1 and has(i - 1, NT):
                    keep_gT(ROUTED_BASE, i - 1, near - 1)

            pipeline(dve, SHARED_FIRST, shared_run(0, 0, SHARED_FIRST))
            pipeline(dve, NT, routed)
            pipeline(dve, T - SHARED_FIRST, shared_run(SHARED_BASE, SHARED_FIRST, T - SHARED_FIRST))
            dve.wait_ge(y_read, SHARED_BASE + T - SHARED_FIRST)
            for q in range(4):
                tiles = slice(8 * q, 8 * q + 8)
                dve.wait_ge(gathered_in[q], 16 * 8)
                dve.tensor_tensor(x_sb[:, tiles, :], gathered[:, tiles, :], x_sb[:, tiles, :], ALU.add
                                  ).then_inc(final_ready, 1)


_INS = ["L0_attn_x", "L0_attn_w_q", "L0_attn_w_k", "L0_attn_w_v", "L0_attn_w_o", "L0_ffn_router_DE",
        "L0_ffn_w1_eDF", "L0_ffn_w3_eDF", "L0_ffn_w2_eFD", "L0_ffn_ws1_DF", "L0_ffn_ws3_DF", "L0_ffn_ws2_FD"]
_OUTS = [((B, S, D), "float32")]


def kernel(**inputs):
    import numpy as np
    import concourse.bacc as bacc
    from concourse.bass_utils import run_bass_kernel_spmd as run

    nc = bacc.Bacc("TRN2", target_bir_lowering=False, num_devices=1)
    arrays, args = {}, []
    for name in _INS:
        a = np.ascontiguousarray(inputs[name])
        arrays[name] = a
        args.append(nc.dram_tensor(name, a.shape, mybir.dt.from_np(a.dtype), kind="ExternalInput").ap())
    outs = []
    for i, (shape, dtype) in enumerate(_OUTS):
        dt = mybir.dt.from_np(np.dtype(dtype))
        outs.append(nc.dram_tensor(f"out_{i}", shape, dt, kind="ExternalOutput").ap())
    preln_attention_moe_kernel(nc, *args, *outs)
    r = run(nc, [arrays], core_ids=[0])
    return r.results[0]["out_0"]
```

```python
import struct
from contextlib import ExitStack

import concourse.bass as bass
from concourse import mybir

F32 = mybir.dt.float32
BF16 = mybir.dt.bfloat16
ALU = mybir.AluOpType
ACT = mybir.ActivationFunctionType
AX = mybir.AxisListType

P = 128
B, S, D = 4, 1024, 128
H, DH = 16, 8
TB = S // P
T = B * TB
CH = 512
NCH = B * S // CH
CT = CH // P
C0 = S // CH
HG = 4
NG = H // HG
ROWS = 3 * 3 * DH
MROW = 96
STEPS = (S // CH) * TB
AHEAD = 4
UNITS = HG * TB
LEAD = 4
OWN_ORDER = (("T", 0), ("S", 0), ("T", 1), ("T", 2), ("S", 1), ("T", 3))
BORROWED_ORDER = (("T", 0), ("T", 1), ("T", 2), ("S", 0), ("T", 3), ("S", 1))
TWO_ONES = struct.unpack("<f", b"\x80\x3f\x80\x3f")[0]
EPS = 1e-5
E, F = 8, 352
FC = 3
NT = T + E - 1
SHARED_FIRST = 18
ROUTED_BASE = SHARED_FIRST
SHARED_BASE = SHARED_FIRST + NT


def preln_attention_moe_kernel(nc, x_in, w_q, w_k, w_v, w_o, router, w1, w3, w2, ws1, ws3, ws2, out):
    x_tiles = x_in.rearrange("b (t p) d -> p (b t) d", p=P)
    out_tiles = out.rearrange("b (t p) d -> p (b t) d", p=P)
    q_parts = nc.dram_tensor("q_parts", (H, 3 * DH, B * S), BF16, kind="Internal").ap()
    k_parts = nc.dram_tensor("k_parts", (H, 5 * DH, B * S), BF16, kind="Internal").ap()

    x_sorted = nc.dram_tensor("x_sorted", (NT * P, D), F32, kind="Internal").ap()
    y_sorted = nc.dram_tensor("y_sorted", (NT * P, D), F32, kind="Internal").ap()

    with ExitStack() as ctx:
        def sb(name, shape, dt):
            return ctx.enter_context(nc.sbuf_tensor(name, shape, dt))

        def sem(name):
            return ctx.enter_context(nc.semaphore(name))

        x_sb = sb("x_sb", [P, T, D], F32)
        q_aug = sb("q_aug", [P, NG, HG, S], BF16)
        k_aug = sb("k_aug", [P, NG, HG, S], BF16)
        probs = sb("probs", [P, 2, HG, CH], F32)
        xn = sb("xn", [P, T, D], F32)
        attn = sb("attn", [P, T, D], F32)
        xnT = attn[:].rearrange("p t d -> p (t d)")
        v_tok = sb("v_tok", [P, T, D], F32)
        v_aug = sb("v_aug", [P, 2, TB, HG, 32], F32)
        o_rows = sb("o_rows", [P, 2, CH], F32)
        ident = sb("ident", [P, P], F32)
        w_raw = sb("w_raw", [P, 4, P], F32)
        w_T = sb("w_T", [P, 4, P], F32)
        half = HG * CH
        early = probs[:].rearrange("p a h c -> p (a h c)")
        parts = early[:, 0:3 * half // 2].bitcast(BF16).rearrange("p (r a c) -> p r a c", a=3, c=CH)
        resid = early[:, 3 * half // 2:2 * half].rearrange("p (r c) -> p r c", c=CH)
        stats = sb("stats", [P, T, 6], F32)
        mv = sb("mv", [P, T, 2], F32)
        var_eps = sb("var_eps", [P, T], F32)
        std = sb("std", [P, T], F32)
        rstd = sb("rstd", [P, T], F32)
        shift = sb("shift", [P, T], F32)
        newton = sb("newton", [P, T], F32)
        neg_max = sb("neg_max", [P, 2, UNITS], F32)
        max_parts = sb("max_parts", [UNITS, 3, P], BF16)
        max_T = sb("max_T", [UNITS, P], F32)
        out_T = sb("out_T", [P, CH], F32)
        rden = sb("rden", [P, 4, HG], F32)
        attnT = sb("attnT", [P, 2, P], F32)

        w13 = sb("w13", [P, (E + 1) * 2 * F], F32)
        w2_sb = xn[:].rearrange("p t d -> p (t d)")[:, 0:(E + 1) * FC * D]
        router_sb = sb("router_sb", [P, E], F32)
        x2n = v_tok
        x2nT = q_aug[:].rearrange("p a h s -> p (a h s)").bitcast(F32)[:, 0:T * P]
        gated = attn
        gathered = k_aug[:].rearrange("p a h s -> p (a h s)").bitcast(F32)[:, 0:T * P].rearrange(
            "p (t d) -> p t d", d=D)
        ffn = probs[:].rearrange("p a h c -> p (a h c)")

        def piece(start, shape):
            n = 2 * shape
            return ffn[:, start:start + n].rearrange("p (r n) -> p r n", r=2)

        xT_sb = piece(0, P)
        xs_sb = piece(2 * P, P)
        y_sb = piece(4 * P, P)
        silu_sb = piece(6 * P, F)
        g_sb = piece(6 * P + 2 * F, F)
        gT_sb = piece(6 * P + 4 * F, FC * P)
        scratch = k_aug[:].rearrange("p a h s -> p (a h s)").bitcast(F32)[:, T * P:2 * T * P]
        zeros = sb("zeros", [P, P], F32)
        before = sb("before", [P, P], BF16)
        ones = sb("ones", [P, P], BF16)
        expert_no = sb("expert_no", [P, T, E], F32)
        tile_rows = sb("tile_rows", [P, T], F32)
        tile_no = sb("tile_no", [P, NT], F32)
        not_first = sb("not_first", [P, E, T], F32)
        logits = scratch[:, 0 * T * E:1 * T * E].rearrange("p (t e) -> p t e", t=T)
        top = sb("top", [P, T], F32)
        cand = scratch[:, 1 * T * E:2 * T * E].rearrange("p (t e) -> p t e", t=T)
        choice = sb("choice", [P, T], F32)
        onehot = sb("onehot", [P, T, E], BF16)
        cum = scratch[:, 2 * T * E:3 * T * E].rearrange("p (e t) -> p e t", e=E)
        place = scratch[:, 3 * T * E:4 * T * E].rearrange("p (t e) -> p t e", t=T)
        count_cmp = scratch[:, 4 * T * E:5 * T * E].rearrange("p (e t) -> p e t", e=E)
        n_tiles = sb("n_tiles", [P, E], F32)
        last_tile = sb("last_tile", [P, E], F32)
        first_row = sb("first_row", [P, E], F32)
        tile_cmp = sb("tile_cmp", [1, NT, E], F32)
        tile_sum = sb("tile_sum", [1, NT], F32)
        tile_expert = sb("tile_expert", [1, NT], mybir.dt.int32)
        row_f = sb("row_f", [P, T], F32)
        row = sb("row", [P, T], mybir.dt.uint32)
        gate = sb("gate", [P, T], F32)
        gate_e = sb("gate_e", [P, T], F32)

        ps = ctx.enter_context(nc.psum_tensor("ps", [P, 8, CH], F32))
        ST, ACC = 4, 7

        def st_bank(m):
            return ST + m % 3

        def tr_bank(w):
            return 2 * (w % 2)

        x_loaded = [sem(f"x_loaded{i}") for i in range(B)]
        w_loaded = sem("w_loaded")
        ident_zero = sem("ident_zero")
        ident_ready = sem("ident_ready")
        aug_clear = sem("aug_clear")
        vaug_clear = sem("vaug_clear")
        stats_done = sem("stats_done")
        mv_done = sem("mv_done")
        var_done = sem("var_done")
        std_done = sem("std_done")
        rstd_step = sem("rstd_step")
        shift_ready = sem("shift_ready")
        xn_ready = sem("xn_ready")
        wT_psum = sem("wT_psum")
        wT_ready = sem("wT_ready")
        xT_psum = sem("xT_psum")
        xT_ready = sem("xT_ready")
        qk_psum = sem("qk_psum")
        stage_ready = sem("stage_ready")
        part1_ready = sem("part1_ready")
        resid_ready = sem("resid_ready")
        part2_ready = sem("part2_ready")
        part3_ready = sem("part3_ready")
        parts_out = [sem(f"parts_out{i}") for i in range(4)]
        v_psum = sem("v_psum")
        v_ready = sem("v_ready")
        aug_loaded = [sem(f"aug_loaded{i}") for i in range(NG)]
        mrow_loaded = [sem(f"mrow_loaded{i}") for i in range(NG)]
        vaug_ready = sem("vaug_ready")
        s_done = sem("s_done")
        max_done = sem("max_done")
        maxT_psum = sem("maxT_psum")
        max_kept = sem("max_kept")
        max_step = sem("max_step")
        st_done = sem("st_done")
        exp_done = sem("exp_done")
        pv_done = sem("pv_done")
        acc_copied = sem("acc_copied")
        o_psum = sem("o_psum")
        rden_ready = sem("rden_ready")
        out_kept = sem("out_kept")
        norm_done = sem("norm_done")
        aT_psum = sem("aT_psum")
        aT_ready = sem("aT_ready")
        proj_psum = sem("proj_psum")
        x2_ready = sem("x2_ready")
        stored = sem("stored")
        ffn_w_loaded = sem("ffn_w_loaded")
        w2_clear = sem("w2_clear")
        consts = sem("consts")
        zero_rows = sem("zero_rows")
        stats2_done = sem("stats2_done")
        mv2_done = sem("mv2_done")
        var2_done = sem("var2_done")
        std2_done = sem("std2_done")
        x2n_ready = sem("x2n_ready")
        x2T_psum = sem("x2T_psum")
        x2T_ready = sem("x2T_ready")
        logits_psum = sem("logits_psum")
        route_step = sem("route_step")
        top_ready = sem("top_ready")
        gate_exp = sem("gate_exp")
        gate_ready = sem("gate_ready")
        onehot_ready = sem("onehot_ready")
        counts_psum = sem("counts_psum")
        table_ready = sem("table_ready")
        rows_ready = sem("rows_ready")
        gated_ready = sem("gated_ready")
        scattered = sem("scattered")
        xs_loaded = [sem(f"xs_loaded{i}") for i in range(2)]
        xsT_psum = sem("xsT_psum")
        ffn_x_ready = sem("ffn_x_ready")
        h_done = sem("h_done")
        silu_done = sem("silu_done")
        g_ready = sem("g_ready")
        gT_psum = sem("gT_psum")
        gT_ready = sem("gT_ready")
        y_psum = sem("y_psum")
        y_read = sem("y_read")
        y_stored = [sem(f"y_stored{i}") for i in range(2)]
        gathered_in = [sem(f"gathered_in{i}") for i in range(4)]
        final_ready = sem("final_ready")

        block = ctx.enter_context(nc.Block())

        def pipeline(eng, n, position):
            for i in range(4):
                position(i, i)
            turns = (n - 1 - 4) // 2
            with eng.Fori(4, 3 + 2 * turns, 2) as i:
                position(i, 4)
                position(i + 1, 5)
            for i in range(4 + 2 * turns, n + 2):
                position(i, i)

        def load_group(sp, row, g):
            heads = slice(g * HG, (g + 1) * HG)
            tok = bass.ds(row * S, S)
            for c in range(3):
                rows = slice(c * 3 * DH, (c + 1) * 3 * DH)
                sp.dma_start(q_aug[rows, g, :, :],
                             q_parts[heads, :, tok].rearrange("h r t -> r h t")).then_inc(aug_loaded[g], 16)
                sp.dma_start(k_aug[rows, g, :, :],
                             k_parts[heads, c * DH:(c + 3) * DH, tok].rearrange("h r t -> r h t")
                             ).then_inc(aug_loaded[g], 16)

        LOADS = 6 * 16
        MROWS = 3 * 16

        def load_max_rows(sp, g):
            for c in range(3):
                dst = q_aug[MROW + c:MROW + c + 1, g, :, :].rearrange("o h (t q) -> o (h t) q", q=P)
                sp.dma_start(dst, max_parts[:, c, :]
                             ).then_inc(mrow_loaded[g], 16)

        def ring_free(eng, signal, base, i, near):
            if near >= 2:
                eng.wait_ge(signal, base + i - 1)
            elif base:
                eng.wait_ge(signal, base)

        def has(i, n):
            return not isinstance(i, int) or i < n

        @block.sync
        def _(sp):
            def load_x(b):
                sp.dma_start(x_sb[:, b * TB:(b + 1) * TB, :],
                             x_tiles[:, b * TB:(b + 1) * TB, :]).then_inc(x_loaded[b], 16)

            def store_parts(u):
                c, is_k = divmod(u, 2)
                sp.wait_ge(part3_ready, u + 1)
                tok = slice(c * CH, (c + 1) * CH)
                if not is_k:
                    for a in range(3):
                        sp.dma_start(q_parts[:, a * DH:(a + 1) * DH, tok],
                                     parts[:, u % 4, a, :]).then_inc(parts_out[u % 4], 16)
                else:
                    for a in range(5):
                        sp.dma_start(k_parts[:, a * DH:(a + 1) * DH, tok],
                                     parts[:, u % 4, a % 3, :]).then_inc(parts_out[u % 4], 16)

            load_x(0)
            for i, w in enumerate((w_q, w_k, w_v, w_o)):
                sp.dma_start(w_raw[:, i, :], w).then_inc(w_loaded, 16)
            for b in range(1, B):
                load_x(b)
            for u in range(2 * C0):
                store_parts(u)
            for i in range(4):
                sp.wait_ge(parts_out[i], 16 * (3, 5)[i % 2] * C0 // 2)
            for g in range(3):
                sp.wait_ge(aug_clear, 3 * (g + 1))
                load_group(sp, 0, g)
            for u in range(2 * C0, 2 * NCH):
                store_parts(u)
            sp.wait_ge(max_step, 4)
            load_max_rows(sp, 0)
            for i in range(4):
                sp.wait_ge(parts_out[i], 16 * (3, 5)[i % 2] * NCH // 2)
            sp.wait_ge(aug_clear, 3 * NG)
            sp.dma_start(router_sb[:], router).then_inc(ffn_w_loaded, 16)
            w13_v = w13[:].rearrange("p (e k f) -> p e k f", k=2, f=F)
            sp.dma_start(w13_v[:, 0:E, 0, :], w1.rearrange("e d f -> d e f")).then_inc(ffn_w_loaded, 16)
            sp.dma_start(w13_v[:, 0:E, 1, :], w3.rearrange("e d f -> d e f")).then_inc(ffn_w_loaded, 16)
            sp.dma_start(w13_v[:, E, 0, :], ws1).then_inc(ffn_w_loaded, 16)
            sp.dma_start(w13_v[:, E, 1, :], ws3).then_inc(ffn_w_loaded, 16)
            sp.wait_ge(w2_clear, 1)
            w2_v = w2_sb.rearrange("p (e c d) -> p e c d", c=FC, d=D)
            for c in range(FC - 1):
                sp.dma_start(w2_v[:, 0:E, c, :], w2[:, c * P:(c + 1) * P, :].rearrange("e f d -> f e d")
                             ).then_inc(ffn_w_loaded, 16)
                sp.dma_start(w2_v[:, E, c, :], ws2[c * P:(c + 1) * P, :]).then_inc(ffn_w_loaded, 16)
            tail = FC * P - F
            sp.dma_start(w2_v[tail:P, 0:E, FC - 1, :], w2[:, (FC - 1) * P:F, :].rearrange("e f d -> f e d")
                         ).then_inc(ffn_w_loaded, 16)
            sp.dma_start(w2_v[tail:P, E, FC - 1, :], ws2[(FC - 1) * P:F, :]).then_inc(ffn_w_loaded, 16)
            for j in range(NT):
                sp.dma_start(x_sorted[j * P:(j + 1) * P, :], zeros[:]).then_inc(zero_rows, 16)

            def batch_row(b, last):
                for g in range(NG):
                    if not (last and g > 0):
                        if g > 0:
                            sp.wait_ge(st_done, (b * NG + g) * HG * STEPS)
                            load_group(sp, b + 1, g - 1)
                        else:
                            sp.wait_ge(st_done, b * NG * HG * STEPS + 1)
                            load_group(sp, b, 3)
                    if not (last and g == NG - 1):
                        sp.wait_ge(max_step, (b * NG + g + 2) * 4)
                        load_max_rows(sp, (g + 1) % NG)

            with sp.Fori(0, B - 1) as b:
                batch_row(b, False)
            batch_row(B - 1, True)

            sp.wait_ge(scattered, 16 * T)

            def load_sorted(i, near, par):
                sp.dma_start(xs_sb[:, par, :], x_sorted[bass.ds(i * P, P), :]).then_inc(xs_loaded[par], 16)

            for i in range(2):
                sp.dma_start(xs_sb[:, i, :], x_sorted[i * P:(i + 1) * P, :]).then_inc(xs_loaded[i], 16)
            turns = (NT - 2) // 2
            with sp.Fori(2, 1 + 2 * turns, 2) as i:
                for p in range(2):
                    sp.wait_ge(xsT_psum, i + p - 1)
                    sp.dma_start(xs_sb[:, p, :], x_sorted[bass.ds((i + p) * P, P), :]).then_inc(xs_loaded[p], 16)
            for i in range(2 + 2 * turns, NT):
                sp.wait_ge(xsT_psum, i - 1)
                sp.dma_start(xs_sb[:, i % 2, :], x_sorted[i * P:(i + 1) * P, :]).then_inc(xs_loaded[i % 2], 16)
            for q in range(4):
                sp.wait_ge(final_ready, q + 1)
                sp.dma_start(out_tiles[:, 8 * q:8 * q + 8, :], x_sb[:, 8 * q:8 * q + 8, :]).then_inc(stored, 16)
            sp.wait_ge(stored, 16 * 4)

        @block.gpsimd
        def _(pool):
            pool.memset(ident[:], 0.0).then_inc(ident_zero, 1)
            pool.wait_ge(ident_zero, 1)
            pool.affine_select(out=ident[:], in_=ident[:], compare_op=ALU.not_equal, fill=1.0, base=0,
                               pattern=[[-1, P]], channel_multiplier=1).then_inc(ident_ready, 1)
            pool.wait_ge(ident_ready, 1)
            for g in range(NG):
                pool.memset(q_aug[64:P, g, :, :].bitcast(F32), 0.0).then_inc(aug_clear, 1)
                pool.wait_ge(aug_clear, 3 * g + 1)
                pool.memset(k_aug[64:P, g, :, :].bitcast(F32), 0.0).then_inc(aug_clear, 1)
                pool.wait_ge(aug_clear, 3 * g + 2)
                pool.memset(k_aug[MROW:MROW + 3, g, :, :].bitcast(F32), TWO_ONES).then_inc(aug_clear, 1)
                pool.wait_ge(aug_clear, 3 * g + 3)
            pool.memset(v_aug[:], 0.0).then_inc(vaug_clear, 1)
            pool.wait_ge(vaug_clear, 1)
            pool.memset(v_aug[:, :, :, :, DH:DH + 1], 1.0).then_inc(vaug_clear, 1)
            pool.wait_ge(vaug_clear, 2)
            n_consts = 0

            def made(ins):
                nonlocal n_consts
                n_consts += 1
                ins.then_inc(consts, 1)
                pool.wait_ge(consts, n_consts)

            made(pool.memset(zeros[:], 0.0))
            made(pool.memset(ones[:], 1.0))
            made(pool.affine_select(out=before[:], in_=ones[:], compare_op=ALU.is_gt, fill=0.0, base=0,
                                    pattern=[[1, P]], channel_multiplier=-1))
            for t, pattern in ((expert_no, [[0, T], [1, E]]), (tile_rows, [[P, T]]), (tile_no, [[1, NT]])):
                made(pool.iota(t[:], pattern, base=0, channel_multiplier=0, allow_small_or_imprecise_dtypes=True))
            made(pool.memset(not_first[:], 1.0))
            made(pool.memset(not_first[:, :, 0:1], 0.0))

            def copy_v(row, g, slot):
                for j in range(HG):
                    c = (g * HG + j) * DH
                    pool.tensor_copy(v_aug[:, slot, :, j, 0:DH],
                                     v_tok[:, bass.ds(row * TB, TB), c:c + DH]).then_inc(vaug_ready, 1)

            pool.wait_ge(v_ready, C0)
            copy_v(0, 0, 0)
            for c in range(C0, NCH):
                for u in (2 * c, 2 * c + 1):
                    pool.wait_ge(part1_ready, u + 1)
                    pool.tensor_tensor(resid[:, u % 2, :], resid[:, u % 2, :], parts[:, u % 4, 0, :],
                                       ALU.subtract).then_inc(resid_ready, 1)
                for u in (2 * c, 2 * c + 1):
                    pool.wait_ge(part2_ready, u + 1)
                    pool.tensor_tensor(parts[:, u % 4, 2, :], resid[:, u % 2, :], parts[:, u % 4, 1, :],
                                       ALU.subtract).then_inc(part3_ready, 1)
            pool.wait_ge(v_ready, NCH)
            pool.wait_ge(xT_psum, NCH)
            pool.memset(w2_sb.rearrange("p (e c d) -> p e c d", c=FC, d=D)[0:FC * P - F, :, FC - 1, :], 0.0
                        ).then_inc(w2_clear, 1)
            pool.wait_ge(w2_clear, 1)

            def batch_row(b, last):
                for g in range(NG):
                    if last and g == NG - 1:
                        continue
                    if g > 0:
                        pool.wait_ge(pv_done, (b * NG + g) * STEPS)
                    else:
                        pool.wait_ge(pv_done, b * NG * STEPS + 1)
                    copy_v(b + (g + 1) // NG, (g + 1) % NG, (g + 1) % 2)

            with pool.Fori(0, B - 1) as b:
                batch_row(b, False)
            batch_row(B - 1, True)

            pool.wait_ge(zero_rows, 16 * NT)
            pool.wait_ge(rows_ready, 1)
            pool.wait_ge(gated_ready, 1)
            for t in range(T):
                pool.indirect_dma_start(out=x_sorted, out_offset=bass.IndirectOffsetOnAxis(ap=row[:, t:t + 1], axis=0),
                                        in_=gated[:, t, :], in_offset=None).then_inc(scattered, 16)
            pool.wait_ge(y_stored[0], 16 * ((NT + 1) // 2))
            pool.wait_ge(y_stored[1], 16 * (NT // 2))
            for t in range(T):
                pool.indirect_dma_start(out=gathered[:, t, :], out_offset=None, in_=y_sorted,
                                        in_offset=bass.IndirectOffsetOnAxis(ap=row[:, t:t + 1], axis=0)
                                        ).then_inc(gathered_in[t // 8], 16)

        @block.scalar
        def _(act):
            def root(call, tiles):
                act.wait_ge(var_done, call + 1)
                act.activation(std[:, tiles], var_eps[:, tiles], ACT.Sqrt).then_inc(std_done, 1)

            def keep_v(c, bank):
                act.wait_ge(v_psum, c + 1)
                act.activation(v_tok[:, CT * c:CT * (c + 1), :],
                               ps[:, bank, :].rearrange("p (t e) -> p t e", e=P), ACT.Copy).then_inc(v_ready, 1)

            root(0, slice(0, TB))
            act.wait_ge(wT_psum, 1)
            act.activation(w_T[:, 0, :], ps[:, 7, 0:P], ACT.Copy, scale=float(DH) ** -0.5).then_inc(wT_ready, 1)
            act.activation(w_T[:, 1:4, :], ps[:, 7, P:4 * P].rearrange("p (w e) -> p w e", e=P),
                           ACT.Copy).then_inc(wT_ready, 1)
            for c in range(C0):
                for k in range(2):
                    u = 2 * c + k
                    act.wait_ge(qk_psum, u + 1)
                    act.activation(parts[:, u % 4, 0, :], ps[:, 2 + u % 2, :], ACT.Copy).then_inc(part1_ready, 1)
                    act.wait_ge(resid_ready, u + 1)
                    act.activation(parts[:, u % 4, 1, :], resid[:, u % 2, :], ACT.Copy).then_inc(part2_ready, 1)
                keep_v(c, 4 + c % 2)
            root(1, slice(TB, T))

            def normalise(t):
                act.activation(xn[:, t, :], x_sb[:, t, :], ACT.Identity, bias=shift[:, t:t + 1],
                               scale=rstd[:, t:t + 1]).then_inc(xn_ready, 1)

            act.wait_ge(shift_ready, 1)
            for t in range(CT * C0, CT * (C0 + 1)):
                normalise(t)
            for c in range(C0, NCH):
                act.wait_ge(xT_psum, c + 1)
                act.activation(xnT[:, c * CH:(c + 1) * CH], ps[:, 4, :], ACT.Copy).then_inc(xT_ready, 1)
                if c + 1 < NCH:
                    for t in range(CT * (c + 1), CT * (c + 2)):
                        normalise(t)
                for u in (2 * c, 2 * c + 1):
                    act.wait_ge(part3_ready, 4 if u == 4 else u - 1)
                    act.wait_ge(parts_out[u % 4], 16 * (3, 5)[u % 2] * (u // 4))
                    act.wait_ge(qk_psum, u + 1)
                    act.activation(resid[:, u % 2, :], ps[:, 5 + u % 2, :], ACT.Copy).then_inc(stage_ready, 1)
                    act.wait_ge(stage_ready, u - 2 * C0 + 1)
                    act.activation(parts[:, u % 4, 0, :], resid[:, u % 2, :], ACT.Copy).then_inc(part1_ready, 1)
                keep_v(c, 7)
                for u in (2 * c, 2 * c + 1):
                    act.wait_ge(resid_ready, u + 1)
                    act.activation(parts[:, u % 4, 1, :], resid[:, u % 2, :], ACT.Copy).then_inc(part2_ready, 1)
            for i in range(4):
                act.wait_ge(parts_out[i], 16 * (3, 5)[i % 2] * NCH // 2)

            def batch_row(b, last):
                for n in range(NG * STEPS):
                    for j in range(HG):
                        act.wait_ge(st_done, (b * NG * STEPS + n) * HG + j + 1)
                        if n >= 2 and j == 0:
                            act.wait_ge(pv_done, b * NG * STEPS + n - 1)
                        act.activation(probs[:, n % 2, j, :], ps[:, st_bank(n % STEPS * HG + j), :],
                                       ACT.Exp).then_inc(exp_done, 1)
                        if n % TB == 0 and n > 0 and j == 3:
                            copy_acc(b, n // TB - 1)
                copy_acc(b, NG * STEPS // TB - 1)

            def copy_acc(b, half):
                halves = NG * STEPS // TB
                act.wait_ge(pv_done, b * NG * STEPS + (half + 1) * TB)
                if half >= 2:
                    act.wait_ge(o_psum, b * halves + half - 1)
                act.activation(o_rows[:, half % 2, :], ps[:, ACC, :], ACT.Copy).then_inc(acc_copied, 1)

            with act.Fori(0, B - 1) as b:
                batch_row(b, False)
            batch_row(B - 1, True)

            for t in range(T):
                act.wait_ge(aT_psum, t + 1)
                if t >= 2:
                    act.wait_ge(proj_psum, t - 1)
                act.activation(attnT[:, t % 2, :], ps[:, t % 2, 0:P], ACT.Copy).then_inc(aT_ready, 1)

            act.wait_ge(var2_done, 1)
            act.activation(std[:], var_eps[:], ACT.Sqrt).then_inc(std2_done, 1)
            for c in range(NCH):
                act.wait_ge(x2T_psum, c + 1)
                act.activation(x2nT[:, c * CH:(c + 1) * CH], ps[:, c % 2, :], ACT.Copy).then_inc(x2T_ready, 1)
            act.wait_ge(top_ready, 1)
            act.activation(gate_e[:], top[:], ACT.Exp, scale=-1.0).then_inc(gate_exp, 1)

            def silu(base, i, near):
                act.wait_ge(h_done, base + i + 1)
                ring_free(act, g_ready, base, i, near)
                act.activation(silu_sb[:, near % 2, :], ps[:, near % 2, 0:F], ACT.Silu).then_inc(silu_done, 1)

            def place_shared(base, tile, i, near):
                ring_free(act, h_done, base, i, near)
                act.activation(xT_sb[:, near % 2, :], x2nT[:, bass.ds((tile + i) * P, P)], ACT.Copy
                               ).then_inc(ffn_x_ready, 1)

            def place_routed(i, near):
                act.wait_ge(xsT_psum, i + 1)
                ring_free(act, h_done, ROUTED_BASE, i, near)
                act.activation(xT_sb[:, near % 2, :], ps[:, 4, 0:P], ACT.Copy).then_inc(ffn_x_ready, 1)

            def shared_run(base, tile, n):
                def position(i, near):
                    if near == 0:
                        place_shared(base, tile, 0, 0)
                    if has(i + 1, n):
                        place_shared(base, tile, i + 1, near + 1)
                    if has(i, n):
                        silu(base, i, near)
                return position

            def routed(i, near):
                if near == 0:
                    place_routed(0, 0)
                if has(i + 1, NT):
                    place_routed(i + 1, near + 1)
                if has(i, NT):
                    silu(ROUTED_BASE, i, near)
                if near >= 2:
                    p = near % 2
                    act.wait_ge(y_psum, ROUTED_BASE + i - 1)
                    if near >= 4:
                        act.wait_ge(y_stored[p], (i - p - 2) * 8)
                    act.activation(y_sb[:, p, :], ps[:, 7, 0:P], ACT.Copy).then_inc(y_read, 1)
                    act.wait_ge(y_read, ROUTED_BASE + i - 1)
                    act.dma_start(y_sorted[bass.ds((i - 2) * P, P), :], y_sb[:, p, :]).then_inc(y_stored[p], 16)

            pipeline(act, SHARED_FIRST, shared_run(0, 0, SHARED_FIRST))
            pipeline(act, NT, routed)
            pipeline(act, T - SHARED_FIRST, shared_run(SHARED_BASE, SHARED_FIRST, T - SHARED_FIRST))

        @block.tensor
        def _(pe):
            pe.wait_ge(ident_ready, 1)
            pe.wait_ge(w_loaded, 64)
            for i in range(4):
                mm = pe.transpose(ps[:, 7, i * P:(i + 1) * P], w_raw[:, i, :], ident[:])
            mm.then_inc(wT_psum, 1)
            def turn_tokens(c, bank):
                pe.wait_ge(xn_ready, CT * (c + 1))
                for i in range(CT):
                    mm = pe.transpose(ps[:, bank, i * P:(i + 1) * P], xn[:, CT * c + i, :], ident[:])
                mm.then_inc(xT_psum, 1)

            def project_qk(c, k, bank):
                pe.wait_ge(xT_ready, c + 1)
                pe.matmul(ps[:, bank, :], w_T[:, k, :], xnT[:, c * CH:(c + 1) * CH],
                          start=True, stop=True).then_inc(qk_psum, 1)

            def project_v(c, bank):
                for t in range(CT * c, CT * (c + 1)):
                    mm = pe.matmul(ps[:, bank, t % CT * P:(t % CT + 1) * P], xnT[:, t * P:(t + 1) * P], w_T[:, 2, :],
                                   start=True, stop=True)
                mm.then_inc(v_psum, 1)

            for c in range(C0):
                turn_tokens(c, c % 2)
                if c == 0:
                    pe.wait_ge(wT_ready, 2)
                for k in range(2):
                    if c > 0:
                        pe.wait_ge(resid_ready, 2 * c + k - 1)
                    project_qk(c, k, 2 + k)
                project_v(c, 4 + c % 2)

            def prepare(c, stage):
                if stage == 0:
                    if c == C0:
                        pe.wait_ge(v_ready, C0 - 1)
                    else:
                        pe.wait_ge(xT_ready, c)
                    turn_tokens(c, 4)
                elif stage < 3:
                    if c == C0:
                        pe.wait_ge(v_ready, C0)
                    else:
                        pe.wait_ge(stage_ready, 2 * (c - C0) + stage - 2)
                    project_qk(c, stage - 1, 4 + stage)
                else:
                    if c > C0:
                        pe.wait_ge(v_ready, c)
                    project_v(c, 7)

            preparations = [(c, stage) for c in range(C0, NCH) for stage in range(4)]

            def score_unit(row, w):
                g, u = divmod(w, UNITS)
                j, t = divmod(u, TB)
                if u == 0:
                    pe.wait_ge(aug_loaded[g % NG], (row + g // NG + 1) * LOADS)
                for half in range(2):
                    mm = pe.matmul(ps[:, tr_bank(w) + half, :], q_aug[0:MROW, g % NG, j, t * P:(t + 1) * P],
                                   k_aug[0:MROW, g % NG, j, half * CH:(half + 1) * CH], start=True, stop=True)
                mm.then_inc(s_done, 1)

            def scores_T(n, j):
                g, s = divmod(n, STEPS)
                half, t = divmod(s, TB)
                pe.matmul(ps[:, st_bank(s * HG + j), :], k_aug[:, g % NG, j, t * P:(t + 1) * P],
                          q_aug[:, g % NG, j, half * CH:(half + 1) * CH], start=True, stop=True
                          ).then_inc(st_done, 1)

            def max_transpose(group, parity, w):
                pe.wait_ge(max_done, (group + 1) * UNITS)
                pe.transpose(ps[0:UNITS, tr_bank(w), 0:P], neg_max[:, parity, :], ident[:]).then_inc(maxT_psum, 1)

            def out_transpose(b, half, w):
                pe.wait_ge(acc_copied, b * 2 * NG + half + 1)
                for i in range(4):
                    mm = pe.transpose(ps[:, tr_bank(w), i * P:(i + 1) * P], o_rows[:, half % 2, i * P:(i + 1) * P],
                                      ident[:])
                mm.then_inc(o_psum, 1)

            for c, stage in preparations[:AHEAD]:
                prepare(c, stage)
            pe.wait_ge(xT_ready, C0)
            pe.wait_ge(resid_ready, 2 * C0)
            for w in range(UNITS + 2 * LEAD):
                if w >= 2:
                    pe.wait_ge(max_done, w - 1)
                score_unit(0, w)
                for c, stage in preparations[AHEAD + w * 2 // 3:AHEAD + (w + 1) * 2 // 3]:
                    prepare(c, stage)
            pe.wait_ge(stage_ready, 2 * (NCH - C0))
            pe.wait_ge(v_ready, NCH)
            pe.wait_ge(max_done, UNITS + 2 * LEAD - 1)
            max_transpose(0, 0, UNITS + 2 * LEAD)
            pe.wait_ge(mrow_loaded[0], MROWS)
            for j in range(HG):
                if j == 3:
                    pe.wait_ge(exp_done, 1)
                scores_T(0, j)

            def values(b, n):
                g, s = divmod(n, STEPS)
                half, t = divmod(s, TB)
                if s == 0:
                    pe.wait_ge(vaug_ready, (b * NG + g + 1) * HG)
                if t == 0 and n > 0:
                    pe.wait_ge(acc_copied, b * 2 * NG + n // TB)
                pe.wait_ge(exp_done, (b * NG * STEPS + n + 1) * HG)
                for j in range(HG):
                    mm = pe.matmul(ps[32 * j:32 * j + 32, ACC, :], v_aug[:, g % 2, t, j, :],
                                   probs[:, n % 2, j, :], start=(t == 0), stop=(t == TB - 1),
                                   tile_position=(0, 32 * j))
                mm.then_inc(pv_done, 1)

            def batch_row(b, last):
                per_row = NG * STEPS
                for n in range(per_row):
                    g, s = divmod(n, STEPS)
                    if n == per_row - 1:
                        values(b, n)
                    borrowed = n == 0 or n > 2 and s in (2, TB + 2) or s == STEPS - LEAD + 1
                    for kind, j in (OWN_ORDER, BORROWED_ORDER)[borrowed]:
                        if kind == "T":
                            if last and n == per_row - 1:
                                continue
                            m = (n + 1) % STEPS * HG + j
                            if m == 0:
                                pe.wait_ge(mrow_loaded[(g + 1) % NG], (b + (g + 1) // NG + 1) * MROWS)
                            used = {0: 1, 1: 4, 2: 4}.get(m, 3)
                            pe.wait_ge(exp_done, (b * per_row + n + 1) * HG + j - used + 1)
                            scores_T(n + 1, j)
                        else:
                            w = UNITS + 2 * LEAD + 2 * n + j
                            if last and w >= NG * UNITS:
                                continue
                            pe.wait_ge(max_done, b * NG * UNITS + w - 1)
                            if j == 0 and s in (2, TB + 2) and n > 2:
                                pe.wait_ge(out_kept, b * 2 * NG + n // TB)
                            if j == 0 and n == 0:
                                pe.wait_ge(max_kept, 1)
                            if j == 0 and s == STEPS - LEAD + 1:
                                pe.wait_ge(max_kept, b * NG + g + 2)
                            score_unit(b, w)
                    if n < per_row - 1:
                        values(b, n)
                    w = UNITS + 2 * LEAD + 2 * (n + 1)
                    if s % TB == 1 and n > 1 or s == STEPS - LEAD and not (last and g == NG - 1):
                        pe.wait_ge(max_done, b * NG * UNITS + min(w - 1, NG * UNITS if last else w))
                        if last and g == NG - 1:
                            pe.wait_ge(out_kept, b * 2 * NG + n // TB - 1)
                    if s == STEPS - LEAD and not (last and g == NG - 1):
                        max_transpose(b * NG + g + 1, (g + 1) % 2, w)
                    if s % TB == 1 and n > 1:
                        out_transpose(b, n // TB - 1, w)
                pe.wait_ge(max_done, b * NG * UNITS + min(w - 1, NG * UNITS if last else w))
                if last:
                    pe.wait_ge(out_kept, b * 2 * NG + 2 * NG - 1)
                out_transpose(b, 2 * NG - 1, w)
                if not last:
                    pe.wait_ge(out_kept, b * 2 * NG + 2 * NG)
                pe.wait_ge(acc_copied, b * 2 * NG + 2 * NG)

            with pe.Fori(0, B - 1) as b:
                batch_row(b, False)
            batch_row(B - 1, True)

            for t in range(T):
                if t == 0:
                    pe.wait_ge(norm_done, B * 2 * NG)
                if t >= 2:
                    pe.wait_ge(aT_ready, t - 1)
                pe.transpose(ps[:, t % 2, 0:P], attn[:, t, :], ident[:]).then_inc(aT_psum, 1)
                pe.wait_ge(aT_ready, t + 1)
                if t >= 2:
                    pe.wait_ge(x2_ready, t - 1)
                pe.matmul(ps[:, 2 + t % 2, 0:P], attnT[:, t % 2, :], w_T[:, 3, :],
                          start=True, stop=True).then_inc(proj_psum, 1)

            for c in range(NCH):
                pe.wait_ge(x2n_ready, 4 * c + 4)
                if c >= 2:
                    pe.wait_ge(x2T_ready, c - 1)
                for i in range(4):
                    mm = pe.transpose(ps[:, c % 2, i * P:(i + 1) * P], x2n[:, 4 * c + i, :], ident[:])
                mm.then_inc(x2T_psum, 1)
                pe.wait_ge(x2T_ready, c + 1)
                if c == 0:
                    pe.wait_ge(ffn_w_loaded, 16 * 11)
                for i in range(4):
                    t = 4 * c + i
                    mm = pe.matmul(ps[:, 4, t * E:(t + 1) * E], x2nT[:, t * P:(t + 1) * P], router_sb[:],
                                   start=True, stop=True)
            mm.then_inc(logits_psum, 1)
            pe.wait_ge(onehot_ready, 1)
            flat = onehot[:].rearrange("p t e -> p (t e)")
            pe.matmul(ps[:, 5, 0:T * E], before[:], flat, start=True, stop=True)
            pe.matmul(ps[:, 6, 0:T * E], ones[:], flat, start=True, stop=True).then_inc(counts_psum, 1)
            pe.wait_ge(rows_ready, 1)

            def hidden(base, i, near, expert):
                p = near % 2
                pe.wait_ge(ffn_x_ready, base + i + 1)
                ring_free(pe, g_ready, base, i, near)
                for k in range(2):
                    mm = pe.matmul(ps[:, 2 * k + p, 0:F], xT_sb[:, p, :], w13[:, bass.ds(expert * 2 * F + k * F, F)],
                                   start=True, stop=True)
                mm.then_inc(h_done, 1)

            def turn_g(base, i, near):
                p = near % 2
                pe.wait_ge(g_ready, base + i + 1)
                ring_free(pe, gT_ready, base, i, near)
                for c in range(FC):
                    f = min(c * P, F - P)
                    mm = pe.transpose(ps[:, 5 + p, c * P:(c + 1) * P], g_sb[:, p, f:f + P], ident[:])
                mm.then_inc(gT_psum, 1)

            def outputs(base, i, near, expert):
                pe.wait_ge(gT_ready, base + i + 1)
                if base or near >= 1:
                    pe.wait_ge(y_read, base + i)
                for c in range(FC):
                    mm = pe.matmul(ps[:, 7, 0:D], gT_sb[:, near % 2, c * P:(c + 1) * P],
                                   w2_sb[:, bass.ds((expert * FC + c) * D, D)], start=(c == 0), stop=(c == FC - 1))
                mm.then_inc(y_psum, 1)

            def shared_run(base, n):
                def position(i, near):
                    if has(i, n):
                        hidden(base, i, near, E)
                    if near >= 1 and has(i - 1, n):
                        turn_g(base, i - 1, near - 1)
                    if near >= 2:
                        outputs(base, i - 2, near - 2, E)
                return position

            def turn_x(i, near):
                pe.wait_ge(xs_loaded[near % 2], x_loads(i, near))
                if near >= 1:
                    pe.wait_ge(ffn_x_ready, ROUTED_BASE + i)
                pe.transpose(ps[:, 4, 0:P], xs_sb[:, near % 2, :], ident[:]).then_inc(xsT_psum, 1)

            def x_loads(i, near):
                return (i - near % 2) * 8 + 16

            def expert_of(i):
                return pe.value_load(tile_expert[0:1, bass.ds(i, 1)], min_val=0, max_val=E - 1)

            def routed(i, near):
                if near == 0:
                    turn_x(0, 0)
                if has(i + 1, NT):
                    turn_x(i + 1, near + 1)
                if has(i, NT):
                    hidden(ROUTED_BASE, i, near, expert_of(i))
                if near >= 1 and has(i - 1, NT):
                    turn_g(ROUTED_BASE, i - 1, near - 1)
                if near >= 2:
                    outputs(ROUTED_BASE, i - 2, near - 2, expert_of(i - 2))

            pipeline(pe, SHARED_FIRST, shared_run(0, SHARED_FIRST))
            pe.wait_ge(table_ready, 1)
            pipeline(pe, NT, routed)
            pipeline(pe, T - SHARED_FIRST, shared_run(SHARED_BASE, T - SHARED_FIRST))

        @block.vector
        def _(dve):
            def layer_norm_stats(call, tiles):
                for t in range(*tiles):
                    if t % TB == 0:
                        dve.wait_ge(x_loaded[t // TB], 16)
                    dve.bn_stats(stats[:, t, :], x_sb[:, t, :]).then_inc(stats_done, 1)
                for t in range(*tiles):
                    dve.wait_ge(stats_done, t + 1)
                    dve.bn_aggr(mv[:, t, :], stats[:, t, :]).then_inc(mv_done, 1)
                dve.wait_ge(mv_done, tiles[1])
                part = slice(*tiles)
                dve.tensor_scalar(var_eps[:, part], mv[:, part, 1], EPS, None, ALU.add).then_inc(var_done, 1)
                dve.wait_ge(std_done, call + 1)
                dve.reciprocal(rstd[:, part], std[:, part]).then_inc(rstd_step, 1)
                refine(5 * call, part)

            def refine(base, part):
                r, n = rstd[:, part], newton[:, part]
                dve.wait_ge(rstd_step, base + 1)
                dve.tensor_tensor(n, r, r, ALU.mult).then_inc(rstd_step, 1)
                dve.wait_ge(rstd_step, base + 2)
                dve.tensor_tensor(n, n, var_eps[:, part], ALU.mult).then_inc(rstd_step, 1)
                dve.wait_ge(rstd_step, base + 3)
                dve.tensor_scalar(n, n, -0.5, 1.5, ALU.mult, ALU.add).then_inc(rstd_step, 1)
                dve.wait_ge(rstd_step, base + 4)
                dve.tensor_tensor(r, r, n, ALU.mult).then_inc(rstd_step, 1)
                dve.wait_ge(rstd_step, base + 5)

            layer_norm_stats(0, (0, TB))

            def normalise(t):
                dve.tensor_scalar(xn[:, t, :], x_sb[:, t, :], mv[:, t, 0:1], rstd[:, t:t + 1],
                                  ALU.subtract, ALU.mult).then_inc(xn_ready, 1)

            for t in range(CT):
                normalise(t)
            for c in range(C0):
                dve.wait_ge(xT_psum, c + 1)
                dve.tensor_copy(xnT[:, c * CH:(c + 1) * CH], ps[:, c % 2, :]).then_inc(xT_ready, 1)
                if c + 1 < C0:
                    for t in range(CT * (c + 1), CT * (c + 2)):
                        normalise(t)
                for k in range(2):
                    u = 2 * c + k
                    dve.wait_ge(part1_ready, u + 1)
                    dve.tensor_tensor(resid[:, u % 2, :], ps[:, 2 + u % 2, :], parts[:, u % 4, 0, :],
                                      ALU.subtract).then_inc(resid_ready, 1)
                for k in range(2):
                    u = 2 * c + k
                    dve.wait_ge(part2_ready, u + 1)
                    dve.tensor_tensor(parts[:, u % 4, 2, :], resid[:, u % 2, :], parts[:, u % 4, 1, :],
                                      ALU.subtract).then_inc(part3_ready, 1)
            layer_norm_stats(1, (TB, T))
            dve.scalar_tensor_tensor(out=shift[:, TB:T], in0=mv[:, TB:T, 0], scalar=-1.0, in1=rstd[:, TB:T],
                                     op0=ALU.mult, op1=ALU.mult).then_inc(shift_ready, 1)

            def row_max(base, w):
                dve.wait_ge(s_done, base + w + 1)
                u = w % UNITS
                dve.tensor_reduce(neg_max[:, w // UNITS % 2, u:u + 1], ps[:, tr_bank(w):tr_bank(w) + 2, :],
                                  mybir.AxisListType.XY, ALU.max, negate=True).then_inc(max_done, 1)

            def split_max(group, slot_free, w):
                dve.wait_ge(maxT_psum, group + 1)
                if slot_free is not None:
                    dve.wait_ge(*slot_free)
                if slot_free is not None:
                    dve.wait_ge(max_step, group * 4)
                dve.tensor_copy(max_T[:], ps[0:UNITS, tr_bank(w), 0:P]).then_inc(max_kept, 1)
                dve.wait_ge(max_kept, group + 1)
                dve.tensor_copy(max_parts[:, 0, :], max_T[:]).then_inc(max_step, 1)
                dve.wait_ge(max_step, group * 4 + 1)
                dve.tensor_tensor(max_T[:], max_T[:], max_parts[:, 0, :], ALU.subtract).then_inc(max_step, 1)
                dve.wait_ge(max_step, group * 4 + 2)
                dve.tensor_copy(max_parts[:, 1, :], max_T[:]).then_inc(max_step, 1)
                dve.wait_ge(max_step, group * 4 + 3)
                dve.tensor_tensor(max_parts[:, 2, :], max_T[:], max_parts[:, 1, :],
                                  ALU.subtract).then_inc(max_step, 1)

            for w in range(UNITS + 2 * LEAD):
                row_max(0, w)
            split_max(0, None, UNITS + 2 * LEAD)

            def norm(b, half, w):
                g, q = divmod(half, 2)
                dve.wait_ge(o_psum, b * 2 * NG + half + 1)
                if half > 0:
                    dve.wait_ge(norm_done, b * 2 * NG + half)
                dve.tensor_copy(out_T[:], ps[:, tr_bank(w), :]).then_inc(out_kept, 1)
                dve.wait_ge(out_kept, b * 2 * NG + half + 1)
                src = out_T[:].rearrange("p (t h r) -> p t h r", t=4, h=HG)
                dve.reciprocal(rden[:], src[:, :, :, DH]).then_inc(rden_ready, 1)
                dve.wait_ge(rden_ready, b * 2 * NG + half + 1)
                dst = attn[:, bass.ds(b * TB + 4 * q, 4), g * HG * DH:(g + 1) * HG * DH]
                dve.tensor_tensor(dst.rearrange("p t (h d) -> p t h d", d=DH), src[:, :, :, 0:DH],
                                  rden[:].rearrange("p t (h o) -> p t h o", o=1).broadcast_to([P, 4, HG, DH]),
                                  ALU.mult).then_inc(norm_done, 1)

            def batch_row(b, last):
                for n in range(NG * STEPS):
                    g, s = divmod(n, STEPS)
                    w = UNITS + 2 * LEAD + 2 * n
                    if s == STEPS - LEAD + 1 and not (last and g == NG - 1):
                        split_max(b * NG + g + 1, (mrow_loaded[g], (b + 1) * MROWS), w)
                    if n % TB == 2 and n > 2:
                        norm(b, n // TB - 1, w)
                    for v in (w, w + 1):
                        if not (last and v >= NG * UNITS):
                            row_max(b * NG * UNITS, v)
                norm(b, 2 * NG - 1, w + 2)
                dve.wait_ge(norm_done, (b + 1) * 2 * NG)

            with dve.Fori(0, B - 1) as b:
                batch_row(b, False)
            batch_row(B - 1, True)

            for t in range(T):
                dve.wait_ge(proj_psum, t + 1)
                dve.tensor_tensor(x_sb[:, t, :], ps[:, 2 + t % 2, 0:P], x_sb[:, t, :], ALU.add).then_inc(x2_ready, 1)
                dve.wait_ge(x2_ready, t + 1)
                dve.bn_stats(stats[:, t, :], x_sb[:, t, :]).then_inc(stats2_done, 1)
            for t in range(T):
                dve.wait_ge(stats2_done, t + 1)
                dve.bn_aggr(mv[:, t, :], stats[:, t, :]).then_inc(mv2_done, 1)
            dve.wait_ge(mv2_done, T)
            dve.tensor_scalar(var_eps[:], mv[:, :, 1], EPS, None, ALU.add).then_inc(var2_done, 1)
            dve.wait_ge(std2_done, 1)
            dve.reciprocal(rstd[:], std[:]).then_inc(rstd_step, 1)
            refine(10, slice(0, T))
            for t in range(T):
                dve.tensor_scalar(x2n[:, t, :], x_sb[:, t, :], mv[:, t, 0:1], rstd[:, t:t + 1],
                                  ALU.subtract, ALU.mult).then_inc(x2n_ready, 1)

            def over_experts(a):
                return a.rearrange("p (t o) -> p t o", o=1).broadcast_to([P, T, E])

            def over_tokens(a):
                return a.rearrange("p (o e) -> p o e", o=1).broadcast_to([P, T, E])

            n_steps = 0

            def step(ins):
                nonlocal n_steps
                n_steps += 1
                ins.then_inc(route_step, 1)
                dve.wait_ge(route_step, n_steps)

            dve.wait_ge(consts, 8)
            dve.wait_ge(logits_psum, 1)
            step(dve.tensor_copy(logits.rearrange("p t e -> p (t e)"), ps[:, 4, 0:T * E]))
            dve.tensor_reduce(top[:], logits, AX.X, ALU.max).then_inc(top_ready, 1)
            dve.wait_ge(top_ready, 1)
            step(dve.tensor_tensor(cand, logits, over_experts(top[:]), ALU.not_equal))
            step(dve.scalar_tensor_tensor(out=cand, in0=cand, scalar=float(2 * E), in1=expert_no[:],
                                          op0=ALU.mult, op1=ALU.add))
            step(dve.tensor_reduce(choice[:], cand, AX.X, ALU.min))
            dve.tensor_tensor(onehot[:], cand, over_experts(choice[:]), ALU.is_equal).then_inc(onehot_ready, 1)
            dve.wait_ge(gate_exp, 1)
            step(dve.tensor_scalar(gate_e[:], gate_e[:], 1.0, None, ALU.add))
            step(dve.reciprocal(gate[:], gate_e[:]))
            dve.tensor_tensor(gated[:], x2n[:], gate[:].rearrange("p (t o) -> p t o", o=1).broadcast_to([P, T, D]),
                              ALU.mult).then_inc(gated_ready, 1)
            dve.wait_ge(counts_psum, 1)
            per_tile = ps[:, 6, 0:T * E].rearrange("p (t e) -> p t e", e=E)
            step(dve.tensor_copy(cum, per_tile.rearrange("p t e -> p e t")))
            step(dve.tensor_tensor_scan(cum.rearrange("p e t -> p (e t)"), not_first[:].rearrange("p e t -> p (e t)"),
                                        cum.rearrange("p e t -> p (e t)"), 0.0, ALU.mult, ALU.add))
            step(dve.tensor_tensor(count_cmp, cum[:, :, T - 1:T].broadcast_to([P, E, T]),
                                   tile_rows[:].rearrange("p (o t) -> p o t", o=1).broadcast_to([P, E, T]), ALU.is_gt))
            step(dve.tensor_reduce(n_tiles[:], count_cmp, AX.X, ALU.add))
            step(dve.tensor_tensor_scan(last_tile[:], ones[:, 0:E], n_tiles[:], 0.0, ALU.mult, ALU.add))
            step(dve.tensor_tensor(first_row[:], last_tile[:], n_tiles[:], ALU.subtract))
            step(dve.tensor_scalar(first_row[:], first_row[:], float(P), None, ALU.mult))
            step(dve.tensor_tensor(place, per_tile, cum.rearrange("p e t -> p t e"), ALU.subtract))
            step(dve.scalar_tensor_tensor(out=place, in0=place, scalar=-1.0,
                                          in1=ps[:, 5, 0:T * E].rearrange("p (t e) -> p t e", e=E),
                                          op0=ALU.mult, op1=ALU.add))
            step(dve.tensor_tensor(place, place, over_tokens(first_row[:]), ALU.add))
            step(dve.tensor_tensor(place, place, onehot[:], ALU.mult))
            step(dve.tensor_reduce(row_f[:], place, AX.X, ALU.add))
            dve.tensor_copy(row[:], row_f[:]).then_inc(rows_ready, 1)
            step(dve.tensor_tensor(tile_cmp[:], tile_no[0:1, :].rearrange("p (j o) -> p j o", o=1).broadcast_to([1, NT, E]),
                                   last_tile[0:1, :].rearrange("p (o e) -> p o e", o=1).broadcast_to([1, NT, E]),
                                   ALU.is_ge))
            step(dve.tensor_reduce(tile_sum[:], tile_cmp[:], AX.X, ALU.add))
            dve.tensor_scalar(tile_expert[:], tile_sum[:], float(E - 1), None, ALU.min).then_inc(table_ready, 1)

            def gate_hidden(base, i, near):
                p = near % 2
                dve.wait_ge(silu_done, base + i + 1)
                ring_free(dve, gT_psum, base, i, near)
                dve.tensor_tensor(g_sb[:, p, :], silu_sb[:, p, :], ps[:, 2 + p, 0:F], ALU.mult).then_inc(g_ready, 1)

            def keep_gT(base, i, near):
                p = near % 2
                dve.wait_ge(gT_psum, base + i + 1)
                ring_free(dve, y_psum, base, i, near)
                dve.tensor_copy(gT_sb[:, p, :], ps[:, 5 + p, 0:FC * P]).then_inc(gT_ready, 1)

            def shared_run(base, tile, n):
                def position(i, near):
                    if has(i, n):
                        gate_hidden(base, i, near)
                    if near >= 1 and has(i - 1, n):
                        keep_gT(base, i - 1, near - 1)
                    if near >= 2:
                        dve.wait_ge(y_psum, base + i - 1)
                        x_t = x_sb[:, bass.ds(tile + i - 2, 1), :].rearrange("p o d -> p (o d)")
                        dve.tensor_tensor(x_t, ps[:, 7, 0:D], x_t, ALU.add).then_inc(y_read, 1)
                return position

            def routed(i, near):
                if has(i, NT):
                    gate_hidden(ROUTED_BASE, i, near)
                if near >= 1 and has(i - 1, NT):
                    keep_gT(ROUTED_BASE, i - 1, near - 1)

            pipeline(dve, SHARED_FIRST, shared_run(0, 0, SHARED_FIRST))
            pipeline(dve, NT, routed)
            pipeline(dve, T - SHARED_FIRST, shared_run(SHARED_BASE, SHARED_FIRST, T - SHARED_FIRST))
            dve.wait_ge(y_read, SHARED_BASE + T - SHARED_FIRST)
            for q in range(4):
                tiles = slice(8 * q, 8 * q + 8)
                dve.wait_ge(gathered_in[q], 16 * 8)
                dve.tensor_tensor(x_sb[:, tiles, :], gathered[:, tiles, :], x_sb[:, tiles, :], ALU.add
                                  ).then_inc(final_ready, 1)


_INS = ["L0_attn_x", "L0_attn_w_q", "L0_attn_w_k", "L0_attn_w_v", "L0_attn_w_o", "L0_ffn_router_DE",
        "L0_ffn_w1_eDF", "L0_ffn_w3_eDF", "L0_ffn_w2_eFD", "L0_ffn_ws1_DF", "L0_ffn_ws3_DF", "L0_ffn_ws2_FD"]
_OUTS = [((B, S, D), "float32")]


def kernel(**inputs):
    import numpy as np
    import concourse.bacc as bacc
    from concourse.bass_utils import run_bass_kernel_spmd as run

    nc = bacc.Bacc("TRN2", target_bir_lowering=False, num_devices=1)
    arrays, args = {}, []
    for name in _INS:
        a = np.ascontiguousarray(inputs[name])
        arrays[name] = a
        args.append(nc.dram_tensor(name, a.shape, mybir.dt.from_np(a.dtype), kind="ExternalInput").ap())
    outs = []
    for i, (shape, dtype) in enumerate(_OUTS):
        dt = mybir.dt.from_np(np.dtype(dtype))
        outs.append(nc.dram_tensor(f"out_{i}", shape, dt, kind="ExternalOutput").ap())
    preln_attention_moe_kernel(nc, *args, *outs)
    r = run(nc, [arrays], core_ids=[0])
    return r.results[0]["out_0"]
```

```python
import struct
from contextlib import ExitStack

import concourse.bass as bass
from concourse import mybir

F32 = mybir.dt.float32
BF16 = mybir.dt.bfloat16
ALU = mybir.AluOpType
ACT = mybir.ActivationFunctionType
AX = mybir.AxisListType

P = 128
B, S, D = 4, 1024, 128
H, DH = 16, 8
TB = S // P
T = B * TB
CH = 512
NCH = B * S // CH
CT = CH // P
C0 = S // CH
HG = 4
NG = H // HG
ROWS = 3 * 3 * DH
MROW = 96
STEPS = (S // CH) * TB
AHEAD = 0
UNITS = HG * TB
LEAD = 4
OWN_ORDER = (("T", 0), ("S", 0), ("T", 1), ("T", 2), ("S", 1), ("T", 3))
BORROWED_ORDER = (("T", 0), ("T", 1), ("T", 2), ("S", 0), ("T", 3), ("S", 1))
TWO_ONES = struct.unpack("<f", b"\x80\x3f\x80\x3f")[0]
BESIDE = range(NCH - 1)
ROOT_STEPS = 3 * 4
ROUTE_PARTS = slice(0, (NCH - 2) * CT), slice((NCH - 2) * CT, T)
EPS = 1e-5
E_BITS = 3
E, F = 8, 352
FC = 3
NT = T + E - 1
SHARED_FIRST = 17
GATED_ACT = 12
ROUTED_BASE = SHARED_FIRST
FINAL_PARTS = slice(0, 12), slice(12, 24), slice(24, T - 2), slice(T - 2, T)
LAG = 5
SHARED_BASE = SHARED_FIRST + NT


def preln_attention_moe_kernel(nc, x_in, w_q, w_k, w_v, w_o, router, w1, w3, w2, ws1, ws3, ws2, out):
    x_tiles = x_in.rearrange("b (t p) d -> p (b t) d", p=P)
    out_tiles = out.rearrange("b (t p) d -> p (b t) d", p=P)
    q_parts = nc.dram_tensor("q_parts", (H, 3 * DH, B * S), BF16, kind="Internal").ap()
    k_parts = nc.dram_tensor("k_parts", (H, 5 * DH, B * S), BF16, kind="Internal").ap()

    x_sorted = nc.dram_tensor("x_sorted", (NT * P, D), F32, kind="Internal").ap()
    y_sorted = nc.dram_tensor("y_sorted", (NT * P, D), F32, kind="Internal").ap()

    with ExitStack() as ctx:
        def sb(name, shape, dt):
            return ctx.enter_context(nc.sbuf_tensor(name, shape, dt))

        def sem(name):
            return ctx.enter_context(nc.semaphore(name))

        x_sb = sb("x_sb", [P, T, D], F32)
        q_aug = sb("q_aug", [P, NG, HG, S], BF16)
        k_aug = sb("k_aug", [P, NG, HG, S], BF16)
        probs = sb("probs", [P, 2, HG, CH], F32)
        xn = sb("xn", [P, T, D], F32)
        attn = sb("attn", [P, T, D], F32)
        xnT = attn[:].rearrange("p t d -> p (t d)")
        v_tok = sb("v_tok", [P, T, D], F32)
        v_aug = sb("v_aug", [P, 2, TB, HG, 32], F32)
        o_rows = sb("o_rows", [P, 2, CH], F32)
        ident = sb("ident", [P, P], F32)
        w_raw = sb("w_raw", [P, 4, P], F32)
        w_T = sb("w_T", [P, 4, P], F32)
        half = HG * CH
        early = probs[:].rearrange("p a h c -> p (a h c)")
        parts = early[:, 0:3 * half // 2].bitcast(BF16).rearrange("p (r a c) -> p r a c", a=3, c=CH)
        resid = early[:, 3 * half // 2:2 * half].rearrange("p (r c) -> p r c", c=CH)
        stats = sb("stats", [P, T, 6], F32)
        mv = sb("mv", [P, T, 2], F32)
        var_eps = sb("var_eps", [P, T], F32)
        std = sb("std", [P, T], F32)
        warm = sb("warm", [P, 1], F32)
        rstd = sb("rstd", [P, T], F32)
        shift = sb("shift", [P, T], F32)
        newton = sb("newton", [P, T], F32)
        neg_max = sb("neg_max", [P, 2, UNITS], F32)
        max_parts = sb("max_parts", [UNITS, 3, P], BF16)
        max_T = sb("max_T", [UNITS, P], F32)
        out_T = sb("out_T", [P, CH], F32)
        rden = sb("rden", [P, 4, HG], F32)
        attnT = sb("attnT", [P, 2, CH], F32)

        w13 = sb("w13", [P, (E + 1) * 2 * F], F32)
        w2_sb = xn[:].rearrange("p t d -> p (t d)")[:, 0:(E + 1) * FC * D]
        router_sb = sb("router_sb", [P, E], F32)
        x2n = v_tok
        x2nT = q_aug[:].rearrange("p a h s -> p (a h s)").bitcast(F32)[:, 0:T * P]
        gated = attn
        gathered = k_aug[:].rearrange("p a h s -> p (a h s)").bitcast(F32)[:, 0:T * P].rearrange(
            "p (t d) -> p t d", d=D)
        ffn = probs[:].rearrange("p a h c -> p (a h c)")

        def piece(start, shape):
            n = 2 * shape
            return ffn[:, start:start + n].rearrange("p (r n) -> p r n", r=2)

        xT_sb = piece(0, P)
        xs_sb = piece(2 * P, P)
        y_sb = piece(4 * P, P)
        silu_sb = piece(6 * P, F)
        g_sb = piece(6 * P + 2 * F, F)
        gT_sb = piece(6 * P + 4 * F, FC * P)
        scratch = k_aug[:].rearrange("p a h s -> p (a h s)").bitcast(F32)[:, T * P:2 * T * P]
        zeros = sb("zeros", [P, P], F32)
        not_before = sb("not_before", [P, P], BF16)
        ones = sb("ones", [P, P], BF16)
        expert_no = sb("expert_no", [P, T, E], F32)
        tile_rows = sb("tile_rows", [P, T], F32)
        tile_no = sb("tile_no", [P, NT], F32)
        not_first = sb("not_first", [P, E, T], F32)
        logits = scratch[:, 0 * T * E:1 * T * E].rearrange("p (t e) -> p t e", t=T)
        top = sb("top", [P, T], F32)
        cand = scratch[:, 1 * T * E:2 * T * E].rearrange("p (t e) -> p t e", t=T)
        choice = sb("choice", [P, T], F32)
        onehot = sb("onehot", [P, T, E], BF16)
        cum = scratch[:, 2 * T * E:3 * T * E].rearrange("p (e t) -> p e t", e=E)
        place = scratch[:, 3 * T * E:4 * T * E].rearrange("p (t e) -> p t e", t=T)
        count_cmp = scratch[:, 4 * T * E:5 * T * E].rearrange("p (e t) -> p e t", e=E)
        n_tiles = sb("n_tiles", [P, E], F32)
        last_tile = sb("last_tile", [P, E], F32)
        first_row = sb("first_row", [P, E], F32)
        tile_cmp = sb("tile_cmp", [1, NT, E], F32)
        tile_sum = sb("tile_sum", [1, NT], F32)
        tile_e = sb("tile_e", [1, NT], F32)
        tile_expert = sb("tile_expert", [1, NT], mybir.dt.int32)
        packed = sb("packed", [1, NT - 4], F32)
        four_experts = sb("four_experts", [1, NT - 4], mybir.dt.int32)
        row_f = sb("row_f", [P, T], F32)
        row = sb("row", [P, T], mybir.dt.uint32)
        gate = sb("gate", [P, T], F32)
        gate_e = sb("gate_e", [P, T], F32)

        ps = ctx.enter_context(nc.psum_tensor("ps", [P, 8, CH], F32))
        ST, ACC = 4, 7

        def st_bank(m):
            return ST + m % 3

        def tr_bank(w):
            return 2 * (w % 2)

        x_loaded = [sem(f"x_loaded{i}") for i in range(B)]
        w_loaded = sem("w_loaded")
        ident_zero = sem("ident_zero")
        ident_ready = sem("ident_ready")
        aug_clear = sem("aug_clear")
        vaug_clear = sem("vaug_clear")
        stats_done = sem("stats_done")
        mv_done = sem("mv_done")
        var_done = sem("var_done")
        std_done = sem("std_done")
        rstd_step = sem("rstd_step")
        shift_ready = sem("shift_ready")
        xn_ready = sem("xn_ready")
        wT_psum = sem("wT_psum")
        wT_ready = sem("wT_ready")
        xT_psum = sem("xT_psum")
        xT_ready = sem("xT_ready")
        qk_psum = sem("qk_psum")
        stage_ready = sem("stage_ready")
        part1_ready = sem("part1_ready")
        resid_ready = sem("resid_ready")
        part2_ready = sem("part2_ready")
        part3_ready = sem("part3_ready")
        parts_out = [sem(f"parts_out{i}") for i in range(4)]
        v_psum = sem("v_psum")
        v_ready = sem("v_ready")
        aug_loaded = [sem(f"aug_loaded{i}") for i in range(NG)]
        mrow_loaded = [sem(f"mrow_loaded{i}") for i in range(NG)]
        vaug_ready = sem("vaug_ready")
        s_done = sem("s_done")
        max_done = sem("max_done")
        maxT_psum = sem("maxT_psum")
        max_kept = sem("max_kept")
        max_step = sem("max_step")
        st_done = sem("st_done")
        exp_done = sem("exp_done")
        pv_done = sem("pv_done")
        acc_copied = sem("acc_copied")
        o_psum = sem("o_psum")
        rden_ready = sem("rden_ready")
        out_kept = sem("out_kept")
        norm_done = sem("norm_done")
        aT_psum = sem("aT_psum")
        aT_ready = sem("aT_ready")
        proj_psum = sem("proj_psum")
        x2_ready = sem("x2_ready")
        stored = sem("stored")
        ffn_w_loaded = sem("ffn_w_loaded")
        w2_clear = sem("w2_clear")
        consts = sem("consts")
        zero_rows = sem("zero_rows")
        stats2_done = sem("stats2_done")
        mv2_done = sem("mv2_done")
        var2_done = sem("var2_done")
        bits_ready = sem("bits_ready")
        guess_ready = sem("guess_ready")
        root2_step = sem("root2_step")
        x2n_ready = sem("x2n_ready")
        x2T_psum = sem("x2T_psum")
        x2T_ready = sem("x2T_ready")
        logits_psum = sem("logits_psum")
        logits_read = sem("logits_read")
        route_step = sem("route_step")
        top_ready = sem("top_ready")
        gate_exp = sem("gate_exp")
        gate_ready = sem("gate_ready")
        onehot_ready = sem("onehot_ready")
        counts_psum = sem("counts_psum")
        table_ready = sem("table_ready")
        rows_ready = sem("rows_ready")
        gated_ready = sem("gated_ready")
        gated_pool = sem("gated_pool")
        scattered = sem("scattered")
        xs_loaded = [sem(f"xs_loaded{i}") for i in range(2)]
        xsT_psum = sem("xsT_psum")
        ffn_x_ready = sem("ffn_x_ready")
        h_done = sem("h_done")
        silu_done = sem("silu_done")
        g_ready = sem("g_ready")
        gT_psum = sem("gT_psum")
        gT_ready = sem("gT_ready")
        y_psum = sem("y_psum")
        y_read = sem("y_read")
        y_stored = [sem(f"y_stored{i}") for i in range(2)]
        gathered_in = [sem(f"gathered_in{i}") for i in range(len(FINAL_PARTS))]
        final_ready = sem("final_ready")

        block = ctx.enter_context(nc.Block())

        def pipeline(eng, n, position):
            for i in range(4):
                position(i, i)
            turns = (n - 1 - 4) // 2
            with eng.Fori(4, 3 + 2 * turns, 2) as i:
                position(i, 4)
                position(i + 1, 5)
            for i in range(4 + 2 * turns, n + 2):
                position(i, i)

        def load_group(sp, row, g):
            heads = slice(g * HG, (g + 1) * HG)
            tok = bass.ds(row * S, S)
            for c in range(3):
                rows = slice(c * 3 * DH, (c + 1) * 3 * DH)
                sp.dma_start(q_aug[rows, g, :, :],
                             q_parts[heads, :, tok].rearrange("h r t -> r h t")).then_inc(aug_loaded[g], 16)
                sp.dma_start(k_aug[rows, g, :, :],
                             k_parts[heads, c * DH:(c + 3) * DH, tok].rearrange("h r t -> r h t")
                             ).then_inc(aug_loaded[g], 16)

        LOADS = 6 * 16
        MROWS = 3 * 16

        def load_max_rows(sp, g):
            for c in range(3):
                dst = q_aug[MROW + c:MROW + c + 1, g, :, :].rearrange("o h (t q) -> o (h t) q", q=P)
                sp.dma_start(dst, max_parts[:, c, :]
                             ).then_inc(mrow_loaded[g], 16)

        def ring_free(eng, signal, base, i, near):
            if near >= 2:
                eng.wait_ge(signal, base + i - 1)
            elif base:
                eng.wait_ge(signal, base)

        def has(i, n):
            return not isinstance(i, int) or i < n

        @block.sync
        def _(sp):
            def load_x(b):
                sp.dma_start(x_sb[:, b * TB:(b + 1) * TB, :],
                             x_tiles[:, b * TB:(b + 1) * TB, :]).then_inc(x_loaded[b], 16)

            def store_chunk(c):
                tok = slice(c * CH, (c + 1) * CH)
                for a, ready in enumerate((part1_ready, part2_ready, part3_ready)):
                    q, k = 2 * c, 2 * c + 1
                    sp.wait_ge(ready, q + 1)
                    sp.dma_start(q_parts[:, a * DH:(a + 1) * DH, tok],
                                 parts[:, q % 4, a, :]).then_inc(parts_out[q % 4], 16)
                    sp.wait_ge(ready, k + 1)
                    for place in (a, a + 3) if a < 2 else (a,):
                        sp.dma_start(k_parts[:, place * DH:(place + 1) * DH, tok],
                                     parts[:, k % 4, a, :]).then_inc(parts_out[k % 4], 16)

            load_x(0)
            for i, w in enumerate((w_q, w_k, w_v, w_o)):
                sp.dma_start(w_raw[:, i, :], w).then_inc(w_loaded, 16)
            for b in range(1, B):
                load_x(b)
            for c in range(C0):
                store_chunk(c)
            for i in range(4):
                sp.wait_ge(parts_out[i], 16 * (3, 5)[i % 2] * C0 // 2)
            for g in range(3):
                sp.wait_ge(aug_clear, 3 * (g + 1))
                load_group(sp, 0, g)
            for c in range(C0, NCH - 1):
                store_chunk(c)
            sp.wait_ge(max_step, 4)
            load_max_rows(sp, 0)
            store_chunk(NCH - 1)
            for i in range(4):
                sp.wait_ge(parts_out[i], 16 * (3, 5)[i % 2] * NCH // 2)
            sp.wait_ge(aug_clear, 3 * NG)
            sp.dma_start(router_sb[:], router).then_inc(ffn_w_loaded, 16)
            w13_v = w13[:].rearrange("p (e k f) -> p e k f", k=2, f=F)
            sp.dma_start(w13_v[:, 0:E, 0, :], w1.rearrange("e d f -> d e f")).then_inc(ffn_w_loaded, 16)
            sp.dma_start(w13_v[:, 0:E, 1, :], w3.rearrange("e d f -> d e f")).then_inc(ffn_w_loaded, 16)
            sp.dma_start(w13_v[:, E, 0, :], ws1).then_inc(ffn_w_loaded, 16)
            sp.dma_start(w13_v[:, E, 1, :], ws3).then_inc(ffn_w_loaded, 16)
            sp.wait_ge(w2_clear, 1)
            w2_v = w2_sb.rearrange("p (e c d) -> p e c d", c=FC, d=D)
            for c in range(FC - 1):
                sp.dma_start(w2_v[:, 0:E, c, :], w2[:, c * P:(c + 1) * P, :].rearrange("e f d -> f e d")
                             ).then_inc(ffn_w_loaded, 16)
                sp.dma_start(w2_v[:, E, c, :], ws2[c * P:(c + 1) * P, :]).then_inc(ffn_w_loaded, 16)
            tail = FC * P - F
            sp.dma_start(w2_v[tail:P, 0:E, FC - 1, :], w2[:, (FC - 1) * P:F, :].rearrange("e f d -> f e d")
                         ).then_inc(ffn_w_loaded, 16)
            sp.dma_start(w2_v[tail:P, E, FC - 1, :], ws2[(FC - 1) * P:F, :]).then_inc(ffn_w_loaded, 16)
            for j in range(NT):
                sp.dma_start(x_sorted[j * P:(j + 1) * P, :], zeros[:]).then_inc(zero_rows, 16)

            def batch_row(b, last):
                for g in range(NG):
                    if not (last and g > 0):
                        if g > 0:
                            sp.wait_ge(st_done, (b * NG + g) * HG * STEPS)
                            load_group(sp, b + 1, g - 1)
                        else:
                            sp.wait_ge(st_done, b * NG * HG * STEPS + 1)
                            load_group(sp, b, 3)
                    if not (last and g == NG - 1):
                        sp.wait_ge(max_step, (b * NG + g + 2) * 4)
                        load_max_rows(sp, (g + 1) % NG)

            with sp.Fori(0, B - 1) as b:
                batch_row(b, False)
            batch_row(B - 1, True)

            sp.wait_ge(scattered, 16 * T)

            def load_sorted(i, p):
                sp.dma_start(xs_sb[:, p, :], x_sorted[bass.ds(i * P, P), :]).then_inc(xs_loaded[p], 16)

            def store_y(i, p):
                sp.wait_ge(y_read, ROUTED_BASE + i + 1)
                sp.dma_start(y_sorted[bass.ds(i * P, P), :], y_sb[:, p, :]).then_inc(y_stored[p], 16)

            for i in range(LAG):
                if i >= 2:
                    sp.wait_ge(xsT_psum, i - 1)
                load_sorted(i, i % 2)
            turns = (NT - LAG) // 2
            with sp.Fori(LAG, LAG + 2 * turns - 1, 2) as i:
                for k in range(2):
                    sp.wait_ge(xsT_psum, i + k - 1)
                    load_sorted(i + k, (LAG + k) % 2)
                    store_y(i + k - LAG, k)
            for i in range(LAG + 2 * turns, NT):
                sp.wait_ge(xsT_psum, i - 1)
                load_sorted(i, i % 2)
                store_y(i - LAG, (i - LAG) % 2)
            for i in range(NT - LAG, NT):
                store_y(i, i % 2)
            for k, tiles in enumerate(FINAL_PARTS):
                sp.wait_ge(final_ready, k + 1)
                sp.dma_start(out_tiles[:, tiles, :], x_sb[:, tiles, :]).then_inc(stored, 16)
            sp.wait_ge(stored, 16 * len(FINAL_PARTS))

        @block.gpsimd
        def _(pool):
            pool.memset(ident[:], 0.0).then_inc(ident_zero, 1)
            pool.wait_ge(ident_zero, 1)
            pool.affine_select(out=ident[:], in_=ident[:], compare_op=ALU.not_equal, fill=1.0, base=0,
                               pattern=[[-1, P]], channel_multiplier=1).then_inc(ident_ready, 1)
            pool.wait_ge(ident_ready, 1)
            for g in range(NG):
                pool.memset(q_aug[64:P, g, :, :].bitcast(F32), 0.0).then_inc(aug_clear, 1)
                pool.wait_ge(aug_clear, 3 * g + 1)
                pool.memset(k_aug[64:P, g, :, :].bitcast(F32), 0.0).then_inc(aug_clear, 1)
                pool.wait_ge(aug_clear, 3 * g + 2)
                pool.memset(k_aug[MROW:MROW + 3, g, :, :].bitcast(F32), TWO_ONES).then_inc(aug_clear, 1)
                pool.wait_ge(aug_clear, 3 * g + 3)
            pool.memset(v_aug[:], 0.0).then_inc(vaug_clear, 1)
            pool.wait_ge(vaug_clear, 1)
            pool.memset(v_aug[:, :, :, :, DH:DH + 1], 1.0).then_inc(vaug_clear, 1)
            pool.wait_ge(vaug_clear, 2)
            n_consts = 0

            def made(ins):
                nonlocal n_consts
                n_consts += 1
                ins.then_inc(consts, 1)
                pool.wait_ge(consts, n_consts)

            made(pool.memset(zeros[:], 0.0))
            made(pool.memset(ones[:], 1.0))
            made(pool.affine_select(out=not_before[:], in_=zeros[:], compare_op=ALU.is_gt, fill=-1.0, base=0,
                                    pattern=[[1, P]], channel_multiplier=-1))
            for t, pattern in ((expert_no, [[0, T], [1, E]]), (tile_rows, [[P, T]]), (tile_no, [[1, NT]])):
                made(pool.iota(t[:], pattern, base=0, channel_multiplier=0, allow_small_or_imprecise_dtypes=True))
            made(pool.memset(not_first[:], 1.0))
            made(pool.memset(not_first[:, :, 0:1], 0.0))

            def copy_v(row, g, slot):
                for j in range(HG):
                    c = (g * HG + j) * DH
                    pool.tensor_copy(v_aug[:, slot, :, j, 0:DH],
                                     v_tok[:, bass.ds(row * TB, TB), c:c + DH]).then_inc(vaug_ready, 1)

            pool.wait_ge(v_ready, C0)
            copy_v(0, 0, 0)
            for c in range(C0, NCH):
                for u in (2 * c, 2 * c + 1):
                    pool.wait_ge(part1_ready, u + 1)
                    pool.tensor_tensor(resid[:, u % 2, :], resid[:, u % 2, :], parts[:, u % 4, 0, :],
                                       ALU.subtract).then_inc(resid_ready, 1)
                for u in (2 * c, 2 * c + 1):
                    pool.wait_ge(part2_ready, u + 1)
                    pool.tensor_tensor(parts[:, u % 4, 2, :], resid[:, u % 2, :], parts[:, u % 4, 1, :],
                                       ALU.subtract).then_inc(part3_ready, 1)
            pool.wait_ge(v_ready, NCH)
            pool.wait_ge(xT_psum, NCH)
            pool.memset(w2_sb.rearrange("p (e c d) -> p e c d", c=FC, d=D)[0:FC * P - F, :, FC - 1, :], 0.0
                        ).then_inc(w2_clear, 1)
            pool.wait_ge(w2_clear, 1)

            def batch_row(b, last):
                for g in range(NG):
                    if last and g == NG - 1:
                        continue
                    if g > 0:
                        pool.wait_ge(pv_done, (b * NG + g) * STEPS)
                    else:
                        pool.wait_ge(pv_done, b * NG * STEPS + 1)
                    copy_v(b + (g + 1) // NG, (g + 1) % NG, (g + 1) % 2)

            with pool.Fori(0, B - 1) as b:
                batch_row(b, False)
            batch_row(B - 1, True)

            for c in BESIDE:
                tiles = slice(CT * c, CT * (c + 1))
                v, r, n = var_eps[:, tiles], rstd[:, tiles], newton[:, tiles]
                pool.wait_ge(guess_ready, c + 1)
                for i in range(3):
                    done = ROOT_STEPS * c + 4 * i
                    pool.tensor_tensor(n, r, r, ALU.mult).then_inc(root2_step, 1)
                    pool.wait_ge(root2_step, done + 1)
                    pool.tensor_tensor(n, n, v, ALU.mult).then_inc(root2_step, 1)
                    pool.wait_ge(root2_step, done + 2)
                    pool.tensor_scalar(n, n, -0.5, 1.5, ALU.mult, ALU.add).then_inc(root2_step, 1)
                    pool.wait_ge(root2_step, done + 3)
                    pool.tensor_tensor(r, r, n, ALU.mult).then_inc(root2_step, 1)
                    pool.wait_ge(root2_step, done + 4)
            pool.wait_ge(gate_ready, 1)
            pool.tensor_tensor(gated[:, GATED_ACT:T, :], x2n[:, GATED_ACT:T, :],
                               gate[:, GATED_ACT:T].rearrange("p (t o) -> p t o", o=1).broadcast_to([P, T - GATED_ACT, D]),
                               ALU.mult).then_inc(gated_pool, 1)
            pool.wait_ge(gated_pool, 1)
            pool.wait_ge(zero_rows, 16 * NT)
            pool.wait_ge(rows_ready, 1)
            for t in (*range(GATED_ACT, T), *range(GATED_ACT)):
                if t == 0:
                    pool.wait_ge(gated_ready, GATED_ACT)
                pool.indirect_dma_start(out=x_sorted, out_offset=bass.IndirectOffsetOnAxis(ap=row[:, t:t + 1], axis=0),
                                        in_=gated[:, t, :], in_offset=None).then_inc(scattered, 16)
            pool.wait_ge(y_stored[0], 16 * ((NT + 1) // 2))
            pool.wait_ge(y_stored[1], 16 * (NT // 2))
            for k, tiles in enumerate(FINAL_PARTS):
                for t in range(tiles.start, tiles.stop):
                    pool.indirect_dma_start(out=gathered[:, t, :], out_offset=None, in_=y_sorted,
                                            in_offset=bass.IndirectOffsetOnAxis(ap=row[:, t:t + 1], axis=0)
                                            ).then_inc(gathered_in[k], 16)

        @block.scalar
        def _(act):
            def root(call, tiles):
                act.wait_ge(var_done, call + 1)
                act.activation(std[:, tiles], var_eps[:, tiles], ACT.Sqrt).then_inc(std_done, 1)

            def keep_v(c, bank):
                act.wait_ge(v_psum, c + 1)
                act.activation(v_tok[:, CT * c:CT * (c + 1), :],
                               ps[:, bank, :].rearrange("p (t e) -> p t e", e=P), ACT.Copy).then_inc(v_ready, 1)

            root(0, slice(0, TB))
            act.wait_ge(wT_psum, 1)
            act.activation(w_T[:, 0, :], ps[:, 7, 0:P], ACT.Copy, scale=float(DH) ** -0.5).then_inc(wT_ready, 1)
            act.activation(w_T[:, 1:4, :], ps[:, 7, P:4 * P].rearrange("p (w e) -> p w e", e=P),
                           ACT.Copy).then_inc(wT_ready, 1)
            for c in range(C0):
                for u in (2 * c, 2 * c + 1):
                    act.wait_ge(qk_psum, u + 1)
                    act.activation(parts[:, u % 4, 0, :], ps[:, 2 + u % 2, :], ACT.Copy).then_inc(part1_ready, 1)
                for u in (2 * c, 2 * c + 1):
                    act.wait_ge(resid_ready, u + 1)
                    act.activation(parts[:, u % 4, 1, :], resid[:, u % 2, :], ACT.Copy).then_inc(part2_ready, 1)
                keep_v(c, 4 + c % 2)
            root(1, slice(TB, T))

            def normalise(t):
                act.activation(xn[:, t, :], x_sb[:, t, :], ACT.Identity, bias=shift[:, t:t + 1],
                               scale=rstd[:, t:t + 1]).then_inc(xn_ready, 1)

            act.wait_ge(shift_ready, 1)
            for t in range(CT * C0, CT * (C0 + 1)):
                normalise(t)
            for c in range(C0, NCH):
                act.wait_ge(xT_psum, c + 1)
                act.activation(xnT[:, c * CH:(c + 1) * CH], ps[:, 4, :], ACT.Copy).then_inc(xT_ready, 1)
                if c + 1 < NCH:
                    for t in range(CT * (c + 1), CT * (c + 2)):
                        normalise(t)
                for u in (2 * c, 2 * c + 1):
                    act.wait_ge(part3_ready, 4 if u == 4 else u - 1)
                    act.wait_ge(parts_out[u % 4], 16 * (3, 5)[u % 2] * (u // 4))
                    act.wait_ge(qk_psum, u + 1)
                    act.activation(resid[:, u % 2, :], ps[:, 5 + u % 2, :], ACT.Copy).then_inc(stage_ready, 1)
                    act.wait_ge(stage_ready, u - 2 * C0 + 1)
                    act.activation(parts[:, u % 4, 0, :], resid[:, u % 2, :], ACT.Copy).then_inc(part1_ready, 1)
                keep_v(c, 7)
                for u in (2 * c, 2 * c + 1):
                    act.wait_ge(resid_ready, u + 1)
                    act.activation(parts[:, u % 4, 1, :], resid[:, u % 2, :], ACT.Copy).then_inc(part2_ready, 1)
            act.activation(warm[:], ident[:, 0:1], ACT.Exp)
            def parts_gone(i):
                act.wait_ge(parts_out[i], 16 * (3, 5)[i % 2] * NCH // 2)

            over_parts = {(0, 0): 0, (0, 1): 1, (0, 3): 2, (1, 0): 3}

            def batch_row(b, first, last):
                for n in range(NG * STEPS):
                    for j in range(HG):
                        act.wait_ge(st_done, (b * NG * STEPS + n) * HG + j + 1)
                        if j == 0 and not (first and n < 2):
                            act.wait_ge(pv_done, b * NG * STEPS + n - 1)
                        if first and (n, j) in over_parts:
                            parts_gone(over_parts[n, j])
                        act.activation(probs[:, n % 2, j, :], ps[:, st_bank(n % STEPS * HG + j), :],
                                       ACT.Exp).then_inc(exp_done, 1)
                        if n % TB == 0 and j == 3:
                            if n >= TB:
                                copy_acc(b, first, n // TB - 1)
                            elif not first:
                                copy_acc(b - 1, False, 2 * NG - 1)
                        s = n - (NG - 1) * STEPS
                        if last and s >= 0 and j == 2:
                            if s % 2 and (s - 1) // 2 in BESIDE:
                                keep_attnT((s - 1) // 2, 1)
                if last:
                    copy_acc(b, False, 2 * NG - 1)

            def keep_attnT(c, bank):
                act.wait_ge(aT_psum, c + 1)
                if c >= 2:
                    act.wait_ge(proj_psum, c - 1)
                act.activation(attnT[:, c % 2, :], ps[:, bank, :], ACT.Copy).then_inc(aT_ready, 1)

            def gate_rows(tiles):
                act.wait_ge(gate_ready, 1)
                for t in tiles:
                    act.activation(gated[:, t, :], x2n[:, t, :], ACT.Copy, scale=gate[:, t:t + 1]
                                   ).then_inc(gated_ready, 1)

            def keep_x2nT(c, bank):
                act.wait_ge(x2T_psum, c + 1)
                act.activation(x2nT[:, c * CH:(c + 1) * CH], ps[:, bank, :], ACT.Copy).then_inc(x2T_ready, 1)

            def copy_acc(b, first, half):
                halves = NG * STEPS // TB
                act.wait_ge(pv_done, b * NG * STEPS + (half + 1) * TB)
                if half >= 2 or not first:
                    act.wait_ge(o_psum, b * halves + half - 1)
                act.activation(o_rows[:, half % 2, :], ps[:, ACC, :], ACT.Copy).then_inc(acc_copied, 1)

            batch_row(0, True, False)
            with act.Fori(1, B - 1) as b:
                batch_row(b, False, False)
            batch_row(B - 1, False, True)

            keep_attnT(NCH - 1, 4)
            keep_x2nT(NCH - 2, 1)
            keep_x2nT(NCH - 1, 4)
            act.wait_ge(top_ready, 2)
            act.activation(gate_e[:], top[:], ACT.Exp, scale=-1.0).then_inc(gate_exp, 1)

            def silu(base, i, near):
                act.wait_ge(h_done, base + i + 1)
                ring_free(act, g_ready, base, i, near)
                act.activation(silu_sb[:, near % 2, :], ps[:, near % 2, 0:F], ACT.Silu).then_inc(silu_done, 1)

            def place_shared(base, tile, i, near):
                ring_free(act, h_done, base, i, near)
                act.activation(xT_sb[:, near % 2, :], x2nT[:, bass.ds((tile + i) * P, P)], ACT.Copy
                               ).then_inc(ffn_x_ready, 1)

            def place_routed(i, near):
                act.wait_ge(xsT_psum, i + 1)
                ring_free(act, h_done, ROUTED_BASE, i, near)
                act.activation(xT_sb[:, near % 2, :], ps[:, 4, 0:P], ACT.Copy).then_inc(ffn_x_ready, 1)

            def shared_run(base, tile, n):
                def position(i, near):
                    if near == 0:
                        place_shared(base, tile, 0, 0)
                    if has(i + 1, n):
                        place_shared(base, tile, i + 1, near + 1)
                    if has(i, n):
                        silu(base, i, near)
                    if base == 0 and isinstance(i, int) and i < 4:
                        gate_rows(range(i * GATED_ACT // 4, (i + 1) * GATED_ACT // 4))
                return position

            def routed(i, near):
                if near == 0:
                    place_routed(0, 0)
                if has(i + 1, NT):
                    place_routed(i + 1, near + 1)
                if has(i, NT):
                    silu(ROUTED_BASE, i, near)
                if near >= 2:
                    p = near % 2
                    act.wait_ge(y_psum, ROUTED_BASE + i - 1)
                    if near >= 4:
                        act.wait_ge(y_stored[p], (i - p - 2) * 8)
                    act.activation(y_sb[:, p, :], ps[:, 7, 0:P], ACT.Copy).then_inc(y_read, 1)

            pipeline(act, SHARED_FIRST, shared_run(0, 0, SHARED_FIRST))
            pipeline(act, NT, routed)
            pipeline(act, T - SHARED_FIRST, shared_run(SHARED_BASE, SHARED_FIRST, T - SHARED_FIRST))

        @block.tensor
        def _(pe):
            pe.wait_ge(ident_ready, 1)
            pe.wait_ge(w_loaded, 64)
            for i in range(4):
                mm = pe.transpose(ps[:, 7, i * P:(i + 1) * P], w_raw[:, i, :], ident[:])
            mm.then_inc(wT_psum, 1)
            def turn_tokens(c, bank):
                pe.wait_ge(xn_ready, CT * (c + 1))
                for i in range(CT):
                    mm = pe.transpose(ps[:, bank, i * P:(i + 1) * P], xn[:, CT * c + i, :], ident[:])
                mm.then_inc(xT_psum, 1)

            def project_qk(c, k, bank):
                pe.wait_ge(xT_ready, c + 1)
                pe.matmul(ps[:, bank, :], w_T[:, k, :], xnT[:, c * CH:(c + 1) * CH],
                          start=True, stop=True).then_inc(qk_psum, 1)

            def project_v(c, bank):
                for t in range(CT * c, CT * (c + 1)):
                    mm = pe.matmul(ps[:, bank, t % CT * P:(t % CT + 1) * P], xnT[:, t * P:(t + 1) * P], w_T[:, 2, :],
                                   start=True, stop=True)
                mm.then_inc(v_psum, 1)

            turn_tokens(0, 0)
            pe.wait_ge(wT_ready, 2)
            for c in range(C0):
                for k in range(2):
                    if c > 0:
                        pe.wait_ge(resid_ready, 2 * c + k - 1)
                    project_qk(c, k, 2 + k)
                if c + 1 < C0:
                    turn_tokens(c + 1, (c + 1) % 2)
                project_v(c, 4 + c % 2)

            def prepare(c, stage):
                if stage == 0:
                    if c == C0:
                        pe.wait_ge(v_ready, C0 - 1)
                    else:
                        pe.wait_ge(xT_ready, c)
                    turn_tokens(c, 4)
                elif stage < 3:
                    if c == C0:
                        pe.wait_ge(v_ready, C0)
                    else:
                        pe.wait_ge(stage_ready, 2 * (c - C0) + stage - 2)
                    project_qk(c, stage - 1, 4 + stage)
                else:
                    if c > C0:
                        pe.wait_ge(v_ready, c)
                    project_v(c, 7)

            preparations = [(c, stage) for c in range(C0, NCH) for stage in range(4)]

            def score_unit(row, w):
                g, u = divmod(w, UNITS)
                j, t = divmod(u, TB)
                if u == 0:
                    pe.wait_ge(aug_loaded[g % NG], (row + g // NG + 1) * LOADS)
                for half in range(2):
                    mm = pe.matmul(ps[:, tr_bank(w) + half, :], q_aug[0:MROW, g % NG, j, t * P:(t + 1) * P],
                                   k_aug[0:MROW, g % NG, j, half * CH:(half + 1) * CH], start=True, stop=True)
                mm.then_inc(s_done, 1)

            def scores_T(n, j):
                g, s = divmod(n, STEPS)
                half, t = divmod(s, TB)
                pe.matmul(ps[:, st_bank(s * HG + j), :], k_aug[:, g % NG, j, t * P:(t + 1) * P],
                          q_aug[:, g % NG, j, half * CH:(half + 1) * CH], start=True, stop=True
                          ).then_inc(st_done, 1)

            def max_transpose(group, parity, w):
                pe.wait_ge(max_done, (group + 1) * UNITS)
                pe.transpose(ps[0:UNITS, tr_bank(w), 0:P], neg_max[:, parity, :], ident[:]).then_inc(maxT_psum, 1)

            def out_transpose(b, half, w):
                pe.wait_ge(acc_copied, b * 2 * NG + half + 1)
                for i in range(4):
                    mm = pe.transpose(ps[:, tr_bank(w), i * P:(i + 1) * P], o_rows[:, half % 2, i * P:(i + 1) * P],
                                      ident[:])
                mm.then_inc(o_psum, 1)

            for c, stage in preparations[:AHEAD]:
                prepare(c, stage)
            pe.wait_ge(xT_ready, C0)
            pe.wait_ge(resid_ready, 2 * C0)
            for w in range(UNITS + 2 * LEAD):
                if w == UNITS:
                    max_transpose(0, 0, UNITS)
                    pe.wait_ge(max_kept, 1)
                elif w >= 2:
                    pe.wait_ge(max_done, w - 1)
                score_unit(0, w)
                for c, stage in preparations[AHEAD + w * 2 // 3:AHEAD + (w + 1) * 2 // 3]:
                    prepare(c, stage)
            pe.wait_ge(stage_ready, 2 * (NCH - C0))
            pe.wait_ge(v_ready, NCH)
            pe.wait_ge(mrow_loaded[0], MROWS)
            for j in range(HG):
                if j == 3:
                    pe.wait_ge(exp_done, 1)
                scores_T(0, j)

            def values(b, first, n):
                g, s = divmod(n, STEPS)
                half, t = divmod(s, TB)
                if s == 0:
                    pe.wait_ge(vaug_ready, (b * NG + g + 1) * HG)
                if t == 0 and not (first and n == 0):
                    pe.wait_ge(acc_copied, b * 2 * NG + n // TB)
                pe.wait_ge(exp_done, (b * NG * STEPS + n + 1) * HG)
                for j in range(HG):
                    mm = pe.matmul(ps[32 * j:32 * j + 32, ACC, :], v_aug[:, g % 2, t, j, :],
                                   probs[:, n % 2, j, :], start=(t == 0), stop=(t == TB - 1),
                                   tile_position=(0, 32 * j))
                mm.then_inc(pv_done, 1)

            def turn_attn(c, bank):
                if c == 0:
                    pe.wait_ge(norm_done, (B - 1) * 2 * NG)
                    pe.wait_ge(max_done, B * NG * UNITS)
                elif c < NCH - 1:
                    pe.wait_ge(aT_ready, c)
                    if c >= 3:
                        pe.wait_ge(x2T_ready, c - 2)
                    if c == NCH - 2:
                        pe.wait_ge(norm_done, B * 2 * NG - 1)
                else:
                    pe.wait_ge(norm_done, B * 2 * NG)
                for i in range(CT):
                    mm = pe.transpose(ps[:, bank, i * P:(i + 1) * P], attn[:, CT * c + i, :], ident[:])
                mm.then_inc(aT_psum, 1)

            def project_out(c, bank):
                pe.wait_ge(aT_ready, c + 1)
                if 0 < c < NCH - 1:
                    pe.wait_ge(x2_ready, c)
                for i in range(CT):
                    mm = pe.matmul(ps[:, bank, i * P:(i + 1) * P], attnT[:, c % 2, i * P:(i + 1) * P],
                                   w_T[:, 3, :], start=True, stop=True)
                mm.then_inc(proj_psum, 1)

            def turn_x2n(c, bank):
                pe.wait_ge(x2n_ready, c + 1)
                if c < NCH - 1:
                    pe.wait_ge(aT_ready, min(c + 3, NCH - 1))
                    if c > 0:
                        pe.wait_ge(x2T_ready, c)
                for i in range(CT):
                    mm = pe.transpose(ps[:, bank, i * P:(i + 1) * P], x2n[:, CT * c + i, :], ident[:])
                mm.then_inc(x2T_psum, 1)

            def route(c):
                pe.wait_ge(x2T_ready, c + 1)
                if c == 0:
                    pe.wait_ge(ffn_w_loaded, 16 * 11)
                for t in range(CT * c, CT * (c + 1)):
                    bank = 3 if t < ROUTE_PARTS[0].stop else 2
                    mm = pe.matmul(ps[:, bank, t * E:(t + 1) * E], x2nT[:, t * P:(t + 1) * P], router_sb[:],
                                   start=True, stop=True)
                if (c + 1) * CT in [tiles.stop for tiles in ROUTE_PARTS]:
                    mm.then_inc(logits_psum, 1)

            def finish_rows_beside(s):
                c, odd = divmod(s, 2)
                if odd:
                    if c in BESIDE:
                        project_out(c, 2)
                    if c - 2 in BESIDE:
                        turn_x2n(c - 2, 1)
                else:
                    if c - 3 in BESIDE:
                        route(c - 3)
                    if c in BESIDE:
                        turn_attn(c, 1)

            def batch_row(b, first, last):
                per_row = NG * STEPS
                for n in range(per_row):
                    g, s = divmod(n, STEPS)
                    turned = s in (2, TB + 2) and not (first and n == 2)
                    borrowed = turned or s == STEPS - LEAD + 1
                    for kind, j in (OWN_ORDER, BORROWED_ORDER)[borrowed]:
                        if last and g == NG - 1 and (kind, j) == ("T", 2):
                            finish_rows_beside(s)
                        if kind == "T":
                            if last and n == per_row - 1:
                                continue
                            m = (n + 1) % STEPS * HG + j
                            if m == 0:
                                pe.wait_ge(mrow_loaded[(g + 1) % NG], (b + (g + 1) // NG + 1) * MROWS)
                            used = {0: 1, 1: 4, 2: 4}.get(m, 3)
                            pe.wait_ge(exp_done, (b * per_row + n + 1) * HG + j - used + 1)
                            scores_T(n + 1, j)
                        else:
                            w = UNITS + 2 * LEAD + 2 * n + j
                            if last and w >= NG * UNITS:
                                continue
                            pe.wait_ge(max_done, b * NG * UNITS + w - 1)
                            if j == 0 and turned:
                                pe.wait_ge(out_kept, b * 2 * NG + n // TB)
                            if j == 0 and s == STEPS - LEAD + 1:
                                pe.wait_ge(max_kept, b * NG + g + 2)
                            score_unit(b, w)
                    values(b, first, n)
                    w = UNITS + 2 * LEAD + 2 * (n + 1)
                    turns = s % TB == 1 and not (first and n == 1)
                    if turns or s == STEPS - LEAD and not (last and g == NG - 1):
                        pe.wait_ge(max_done, b * NG * UNITS + min(w - 1, NG * UNITS if last else w))
                        if last and g == NG - 1:
                            pe.wait_ge(out_kept, b * 2 * NG + n // TB - 1)
                    if s == STEPS - LEAD and not (last and g == NG - 1):
                        max_transpose(b * NG + g + 1, (g + 1) % 2, w)
                    if turns:
                        out_transpose(b, n // TB - 1, w)
                if last:
                    pe.wait_ge(out_kept, b * 2 * NG + 2 * NG - 1)
                    out_transpose(b, 2 * NG - 1, w)

            batch_row(0, True, False)
            with pe.Fori(1, B - 1) as b:
                batch_row(b, False, False)
            batch_row(B - 1, False, True)

            route(NCH - 3)
            pe.wait_ge(exp_done, B * NG * STEPS * HG)
            turn_attn(NCH - 1, 4)
            project_out(NCH - 1, 5)
            turn_x2n(NCH - 2, 1)
            route(NCH - 2)
            turn_x2n(NCH - 1, 4)
            route(NCH - 1)
            pe.wait_ge(logits_read, 2)

            def count_tokens():
                pe.wait_ge(onehot_ready, 2)
                flat = onehot[:].rearrange("p t e -> p (t e)")
                pe.matmul(ps[:, 4, 0:T * E], not_before[:], flat, start=True, stop=True)
                pe.matmul(ps[:, 4, T * E:2 * T * E], ones[:], flat, start=True, stop=True).then_inc(counts_psum, 1)

            def hidden(base, i, near, col):
                p = near % 2
                pe.wait_ge(ffn_x_ready, base + i + 1)
                ring_free(pe, g_ready, base, i, near)
                for k in range(2):
                    mm = pe.matmul(ps[:, 2 * k + p, 0:F], xT_sb[:, p, :], w13[:, k * F:][:, bass.ds(col, F)],
                                   start=True, stop=True)
                mm.then_inc(h_done, 1)

            def turn_g(base, i, near):
                p = near % 2
                pe.wait_ge(g_ready, base + i + 1)
                ring_free(pe, gT_ready, base, i, near)
                for c in range(FC):
                    f = min(c * P, F - P)
                    mm = pe.transpose(ps[:, 5 + p, c * P:(c + 1) * P], g_sb[:, p, f:f + P], ident[:])
                mm.then_inc(gT_psum, 1)

            def outputs(base, i, near, col):
                pe.wait_ge(gT_ready, base + i + 1)
                if base or near >= 1:
                    pe.wait_ge(y_read, base + i)
                for c in range(FC):
                    mm = pe.matmul(ps[:, 7, 0:D], gT_sb[:, near % 2, c * P:(c + 1) * P],
                                   w2_sb[:, c * D:][:, bass.ds(col, D)], start=(c == 0), stop=(c == FC - 1))
                mm.then_inc(y_psum, 1)

            def shared_run(base, n):
                def position(i, near):
                    if base == 0 and near == 0:
                        count_tokens()
                    if has(i, n):
                        hidden(base, i, near, E * 2 * F)
                    if near >= 1 and has(i - 1, n):
                        turn_g(base, i - 1, near - 1)
                    if near >= 2:
                        outputs(base, i - 2, near - 2, E * FC * D)
                return position

            def turn_x(i, near):
                pe.wait_ge(xs_loaded[near % 2], x_loads(i, near))
                if near >= 1:
                    pe.wait_ge(ffn_x_ready, ROUTED_BASE + i)
                pe.transpose(ps[:, 4, 0:P], xs_sb[:, near % 2, :], ident[:]).then_inc(xsT_psum, 1)

            def x_loads(i, near):
                return (i - near % 2) * 8 + 16

            def expert_of(i):
                return pe.value_load(tile_expert[0:1, bass.ds(i, 1)], min_val=0, max_val=E - 1)

            def head(i, near, col):
                if near == 0:
                    turn_x(0, 0)
                if has(i + 1, NT):
                    turn_x(i + 1, near + 1)
                if has(i, NT):
                    hidden(ROUTED_BASE, i, near, col)

            def rest(i, near, col):
                if near >= 1 and has(i - 1, NT):
                    turn_g(ROUTED_BASE, i - 1, near - 1)
                if near >= 2:
                    outputs(ROUTED_BASE, i - 2, near - 2, col)

            def head_alone(i):
                head(i, i, expert_of(i) * (2 * F) if i < NT else None)

            def rest_alone(i):
                rest(i, i, expert_of(i - 2) * (FC * D) if i >= 2 else None)

            def routed_run():
                for i in range(4):
                    head_alone(i)
                    rest_alone(i)
                head_alone(4)
                turns = (NT - 3 - 4) // 2
                with pe.Fori(4, 3 + 2 * turns, 2) as i:
                    four = pe.value_load(four_experts[0:1, bass.ds(i - 2, 1)], min_val=0,
                                         max_val=E ** 4 - 1)

                    def col(k, width):
                        return pe.snap(((four >> (E_BITS * k)) & (E - 1)) * width)

                    cols = col(0, FC * D), col(2, 2 * F), col(1, FC * D), col(3, 2 * F)
                    rest(i, 4, cols[0])
                    head(i + 1, 5, cols[1])
                    rest(i + 1, 5, cols[2])
                    head(i + 2, 6, cols[3])
                rest_alone(4 + 2 * turns)
                for i in range(5 + 2 * turns, NT + 2):
                    head_alone(i)
                    rest_alone(i)

            pipeline(pe, SHARED_FIRST, shared_run(0, SHARED_FIRST))
            pe.wait_ge(table_ready, 2)
            pe.wait_ge(rows_ready, 1)
            routed_run()
            pipeline(pe, T - SHARED_FIRST, shared_run(SHARED_BASE, T - SHARED_FIRST))

        @block.vector
        def _(dve):
            def layer_norm_stats(call, tiles):
                for t in range(*tiles):
                    if t % TB == 0:
                        dve.wait_ge(x_loaded[t // TB], 16)
                    dve.bn_stats(stats[:, t, :], x_sb[:, t, :]).then_inc(stats_done, 1)
                for t in range(*tiles):
                    dve.wait_ge(stats_done, t + 1)
                    dve.bn_aggr(mv[:, t, :], stats[:, t, :]).then_inc(mv_done, 1)
                dve.wait_ge(mv_done, tiles[1])
                part = slice(*tiles)
                dve.tensor_scalar(var_eps[:, part], mv[:, part, 1], EPS, None, ALU.add).then_inc(var_done, 1)
                dve.wait_ge(std_done, call + 1)
                dve.reciprocal(rstd[:, part], std[:, part]).then_inc(rstd_step, 1)
                refine(5 * call, part)

            def refine(base, part):
                r, n = rstd[:, part], newton[:, part]
                dve.wait_ge(rstd_step, base + 1)
                dve.tensor_tensor(n, r, r, ALU.mult).then_inc(rstd_step, 1)
                dve.wait_ge(rstd_step, base + 2)
                dve.tensor_tensor(n, n, var_eps[:, part], ALU.mult).then_inc(rstd_step, 1)
                dve.wait_ge(rstd_step, base + 3)
                dve.tensor_scalar(n, n, -0.5, 1.5, ALU.mult, ALU.add).then_inc(rstd_step, 1)
                dve.wait_ge(rstd_step, base + 4)
                dve.tensor_tensor(r, r, n, ALU.mult).then_inc(rstd_step, 1)
                dve.wait_ge(rstd_step, base + 5)

            layer_norm_stats(0, (0, TB))

            def normalise(t):
                dve.tensor_scalar(xn[:, t, :], x_sb[:, t, :], mv[:, t, 0:1], rstd[:, t:t + 1],
                                  ALU.subtract, ALU.mult).then_inc(xn_ready, 1)

            def keep_xT(c):
                dve.wait_ge(xT_psum, c + 1)
                dve.tensor_copy(xnT[:, c * CH:(c + 1) * CH], ps[:, c % 2, :]).then_inc(xT_ready, 1)
                if c + 1 < C0:
                    for t in range(CT * (c + 1), CT * (c + 2)):
                        normalise(t)

            for t in range(CT):
                normalise(t)
            keep_xT(0)
            for c in range(C0):
                for u in (2 * c, 2 * c + 1):
                    if u >= 2:
                        dve.wait_ge(part3_ready, u - 1)
                    dve.wait_ge(part1_ready, u + 1)
                    dve.tensor_tensor(resid[:, u % 2, :], ps[:, 2 + u % 2, :], parts[:, u % 4, 0, :],
                                      ALU.subtract).then_inc(resid_ready, 1)
                if c + 1 < C0:
                    keep_xT(c + 1)
                for u in (2 * c, 2 * c + 1):
                    dve.wait_ge(part2_ready, u + 1)
                    dve.tensor_tensor(parts[:, u % 4, 2, :], resid[:, u % 2, :], parts[:, u % 4, 1, :],
                                      ALU.subtract).then_inc(part3_ready, 1)
            layer_norm_stats(1, (TB, T))
            dve.scalar_tensor_tensor(out=shift[:, TB:T], in0=mv[:, TB:T, 0], scalar=-1.0, in1=rstd[:, TB:T],
                                     op0=ALU.mult, op1=ALU.mult).then_inc(shift_ready, 1)

            def row_max(base, w):
                dve.wait_ge(s_done, base + w + 1)
                u = w % UNITS
                dve.tensor_reduce(neg_max[:, w // UNITS % 2, u:u + 1], ps[:, tr_bank(w):tr_bank(w) + 2, :],
                                  mybir.AxisListType.XY, ALU.max, negate=True).then_inc(max_done, 1)

            def split_max(group, slot_free, w):
                dve.wait_ge(maxT_psum, group + 1)
                if slot_free is not None:
                    dve.wait_ge(*slot_free)
                if slot_free is not None:
                    dve.wait_ge(max_step, group * 4)
                dve.tensor_copy(max_T[:], ps[0:UNITS, tr_bank(w), 0:P]).then_inc(max_kept, 1)
                dve.wait_ge(max_kept, group + 1)
                dve.tensor_copy(max_parts[:, 0, :], max_T[:]).then_inc(max_step, 1)
                dve.wait_ge(max_step, group * 4 + 1)
                dve.tensor_tensor(max_T[:], max_T[:], max_parts[:, 0, :], ALU.subtract).then_inc(max_step, 1)
                dve.wait_ge(max_step, group * 4 + 2)
                dve.tensor_copy(max_parts[:, 1, :], max_T[:]).then_inc(max_step, 1)
                dve.wait_ge(max_step, group * 4 + 3)
                dve.tensor_tensor(max_parts[:, 2, :], max_T[:], max_parts[:, 1, :],
                                  ALU.subtract).then_inc(max_step, 1)

            for w in range(UNITS + 2 * LEAD):
                if w == UNITS:
                    split_max(0, None, UNITS)
                row_max(0, w)

            def norm(b, first, half, w):
                g, q = divmod(half, 2)
                dve.wait_ge(o_psum, b * 2 * NG + half + 1)
                if half > 0 or not first:
                    dve.wait_ge(norm_done, b * 2 * NG + half)
                dve.tensor_copy(out_T[:], ps[:, tr_bank(w), :]).then_inc(out_kept, 1)
                dve.wait_ge(out_kept, b * 2 * NG + half + 1)
                src = out_T[:].rearrange("p (t h r) -> p t h r", t=4, h=HG)
                dve.reciprocal(rden[:], src[:, :, :, DH]).then_inc(rden_ready, 1)
                dve.wait_ge(rden_ready, b * 2 * NG + half + 1)
                dst = attn[:, bass.ds(b * TB + 4 * q, 4), g * HG * DH:(g + 1) * HG * DH]
                dve.tensor_tensor(dst.rearrange("p t (h d) -> p t h d", d=DH), src[:, :, :, 0:DH],
                                  rden[:].rearrange("p t (h o) -> p t h o", o=1).broadcast_to([P, 4, HG, DH]),
                                  ALU.mult).then_inc(norm_done, 1)

            def sum_rows(c, bank):
                tiles = slice(CT * c, CT * (c + 1))
                dve.wait_ge(proj_psum, c + 1)
                x_c = x_sb[:, tiles, :].rearrange("p t d -> p (t d)")
                dve.tensor_tensor(x_c, ps[:, bank, :], x_c, ALU.add).then_inc(x2_ready, 1)
                dve.wait_ge(x2_ready, c + 1)
                for t in range(CT * c, CT * (c + 1)):
                    dve.bn_stats(stats[:, t, :], x_sb[:, t, :]).then_inc(stats2_done, 1)
                for t in range(CT * c, CT * (c + 1)):
                    dve.wait_ge(stats2_done, t + 1)
                    dve.bn_aggr(mv[:, t, :], stats[:, t, :]).then_inc(mv2_done, 1)
                dve.wait_ge(mv2_done, CT * (c + 1))
                v = var_eps[:, tiles]
                dve.tensor_scalar(v, mv[:, tiles, 1], EPS, None, ALU.add).then_inc(var2_done, 1)
                dve.wait_ge(var2_done, c + 1)
                bits = rstd[:, tiles].bitcast(mybir.dt.int32)
                dve.tensor_scalar(bits, v.bitcast(mybir.dt.int32), 1, None, ALU.logical_shift_right
                                  ).then_inc(bits_ready, 1)
                dve.wait_ge(bits_ready, c + 1)
                dve.tensor_scalar(bits, bits, -1, 0x5F3759DF, ALU.mult, ALU.add).then_inc(guess_ready, 1)

            def keep_x2nT(c):
                dve.wait_ge(x2T_psum, c + 1)
                dve.tensor_copy(x2nT[:, c * CH:(c + 1) * CH], ps[:, 1, :]).then_inc(x2T_ready, 1)

            def normalise_rows(c):
                if c in BESIDE:
                    dve.wait_ge(root2_step, ROOT_STEPS * (c + 1))
                for t in range(CT * c, CT * (c + 1)):
                    ins = dve.tensor_scalar(x2n[:, t, :], x_sb[:, t, :], mv[:, t, 0:1], rstd[:, t:t + 1],
                                            ALU.subtract, ALU.mult)
                ins.then_inc(x2n_ready, 1)

            def beside(c):
                if c >= 1:
                    normalise_rows(c - 1)
                sum_rows(c, 2)

            def batch_row(b, first, last):
                for n in range(NG * STEPS):
                    g, s = divmod(n, STEPS)
                    w = UNITS + 2 * LEAD + 2 * n
                    if s == STEPS - LEAD + 1 and not (last and g == NG - 1):
                        split_max(b * NG + g + 1, (mrow_loaded[g], (b + 1) * MROWS), w)
                    if last and g == NG - 1 and s % 2 == 0 and s >= 6:
                        keep_x2nT(s // 2 - 3)
                    if n % TB == 2 and n > 2:
                        norm(b, first, n // TB - 1, w)
                    elif n == 2 and not first:
                        norm(b - 1, False, 2 * NG - 1, w)
                    for v in (w, w + 1):
                        if not (last and v >= NG * UNITS):
                            row_max(b * NG * UNITS, v)
                    if last and g == NG - 1 and s % 2 == 0 and s > 0:
                        beside(s // 2 - 1)
                if last:
                    keep_x2nT(NCH - 3)
                    norm(b, False, 2 * NG - 1, w + 2)

            batch_row(0, True, False)
            with dve.Fori(1, B - 1) as b:
                batch_row(b, False, False)
            batch_row(B - 1, False, True)

            n_steps = 0

            def step(ins):
                nonlocal n_steps
                n_steps += 1
                ins.then_inc(route_step, 1)
                dve.wait_ge(route_step, n_steps)

            def over_experts(a):
                return a.rearrange("p (t o) -> p t o", o=1).broadcast_to([P, a.shape[1], E])

            def over_tokens(a):
                return a.rearrange("p (o e) -> p o e", o=1).broadcast_to([P, T, E])

            def choose(k):
                tiles = ROUTE_PARTS[k]
                logit, other = logits[:, tiles, :], cand[:, tiles, :]
                dve.wait_ge(logits_psum, k + 1)
                dve.tensor_copy(logit.rearrange("p t e -> p (t e)"), ps[:, 3 - k, tiles.start * E:tiles.stop * E]
                                ).then_inc(logits_read, 1)
                dve.wait_ge(logits_read, k + 1)
                dve.tensor_reduce(top[:, tiles], logit, AX.X, ALU.max).then_inc(top_ready, 1)
                dve.wait_ge(top_ready, k + 1)
                step(dve.tensor_tensor(other, logit, over_experts(top[:, tiles]), ALU.not_equal))
                step(dve.scalar_tensor_tensor(out=other, in0=other, scalar=float(2 * E), in1=expert_no[:, tiles, :],
                                              op0=ALU.mult, op1=ALU.add))
                step(dve.tensor_reduce(choice[:, tiles], other, AX.X, ALU.min))
                dve.tensor_tensor(onehot[:, tiles, :], other, over_experts(choice[:, tiles]), ALU.is_equal
                                  ).then_inc(onehot_ready, 1)

            dve.wait_ge(consts, 8)
            normalise_rows(NCH - 2)
            sum_rows(NCH - 1, 5)
            dve.wait_ge(guess_ready, NCH)
            tiles = slice(T - CT, T)
            v, r, n = var_eps[:, tiles], rstd[:, tiles], newton[:, tiles]
            for _ in range(3):
                step(dve.scalar_tensor_tensor(out=n, in0=r, scalar=-0.5, in1=r, op0=ALU.mult, op1=ALU.mult))
                step(dve.tensor_tensor(n, n, v, ALU.mult))
                step(dve.scalar_tensor_tensor(out=r, in0=n, scalar=1.5, in1=r, op0=ALU.add, op1=ALU.mult))
            normalise_rows(NCH - 1)
            choose(0)
            choose(1)
            dve.wait_ge(gate_exp, 1)
            step(dve.tensor_scalar(gate_e[:], gate_e[:], 1.0, None, ALU.add))
            dve.reciprocal(gate[:], gate_e[:]).then_inc(gate_ready, 1)

            per_tile = ps[:, 4, T * E:2 * T * E].rearrange("p (t e) -> p t e", e=E)

            def running_counts():
                dve.wait_ge(counts_psum, 1)
                step(dve.tensor_copy(cum, per_tile.rearrange("p t e -> p e t")))
                step(dve.tensor_tensor_scan(cum.rearrange("p e t -> p (e t)"), not_first[:].rearrange("p e t -> p (e t)"),
                                            cum.rearrange("p e t -> p (e t)"), 0.0, ALU.mult, ALU.add))

            def expert_tiles():
                step(dve.tensor_tensor(count_cmp, cum[:, :, T - 1:T].broadcast_to([P, E, T]),
                                       tile_rows[:].rearrange("p (o t) -> p o t", o=1).broadcast_to([P, E, T]), ALU.is_gt))
                step(dve.tensor_reduce(n_tiles[:], count_cmp, AX.X, ALU.add))
                step(dve.tensor_tensor_scan(last_tile[:], ones[:, 0:E], n_tiles[:], 0.0, ALU.mult, ALU.add))
                step(dve.tensor_tensor(first_row[:], last_tile[:], n_tiles[:], ALU.subtract))
                step(dve.tensor_scalar(first_row[:], first_row[:], float(P), None, ALU.mult))

            def token_rows():
                step(dve.tensor_tensor(place, ps[:, 4, 0:T * E].rearrange("p (t e) -> p t e", e=E),
                                       cum.rearrange("p e t -> p t e"), ALU.add))
                step(dve.tensor_tensor(place, place, over_tokens(first_row[:]), ALU.add))
                step(dve.tensor_tensor(place, place, onehot[:], ALU.mult))
                step(dve.tensor_reduce(row_f[:], place, AX.X, ALU.add))
                dve.tensor_copy(row[:], row_f[:]).then_inc(rows_ready, 1)

            def tile_table():
                step(dve.tensor_tensor(tile_cmp[:], tile_no[0:1, :].rearrange("p (j o) -> p j o", o=1).broadcast_to([1, NT, E]),
                                       last_tile[0:1, :].rearrange("p (o e) -> p o e", o=1).broadcast_to([1, NT, E]),
                                       ALU.is_ge))
                step(dve.tensor_reduce(tile_sum[:], tile_cmp[:], AX.X, ALU.add))
                dve.tensor_scalar(tile_expert[:], tile_sum[:], float(E - 1), None, ALU.min).then_inc(table_ready, 1)
                step(dve.tensor_scalar(tile_e[:], tile_sum[:], float(E - 1), None, ALU.min))
                step(dve.scalar_tensor_tensor(out=packed[:], in0=tile_e[0:1, 4:NT], scalar=float(E),
                                              in1=tile_e[0:1, 3:NT - 1], op0=ALU.mult, op1=ALU.add))
                step(dve.scalar_tensor_tensor(out=packed[:], in0=packed[:], scalar=float(E),
                                              in1=tile_e[0:1, 1:NT - 3], op0=ALU.mult, op1=ALU.add))
                dve.scalar_tensor_tensor(out=four_experts[:], in0=packed[:], scalar=float(E),
                                         in1=tile_e[0:1, 0:NT - 4], op0=ALU.mult, op1=ALU.add).then_inc(table_ready, 1)

            def gate_hidden(base, i, near):
                p = near % 2
                dve.wait_ge(silu_done, base + i + 1)
                ring_free(dve, gT_psum, base, i, near)
                dve.tensor_tensor(g_sb[:, p, :], silu_sb[:, p, :], ps[:, 2 + p, 0:F], ALU.mult).then_inc(g_ready, 1)

            def keep_gT(base, i, near):
                p = near % 2
                dve.wait_ge(gT_psum, base + i + 1)
                ring_free(dve, y_psum, base, i, near)
                dve.tensor_copy(gT_sb[:, p, :], ps[:, 5 + p, 0:FC * P]).then_inc(gT_ready, 1)

            def shared_run(base, tile, n):
                def position(i, near):
                    if has(i, n):
                        gate_hidden(base, i, near)
                    if base == 0:
                        if near == 1:
                            tile_table()
                    if near >= 1 and has(i - 1, n):
                        keep_gT(base, i - 1, near - 1)
                    if near >= 2:
                        dve.wait_ge(y_psum, base + i - 1)
                        x_t = x_sb[:, bass.ds(tile + i - 2, 1), :].rearrange("p o d -> p (o d)")
                        dve.tensor_tensor(x_t, ps[:, 7, 0:D], x_t, ALU.add).then_inc(y_read, 1)
                return position

            def routed(i, near):
                if has(i, NT):
                    gate_hidden(ROUTED_BASE, i, near)
                if near >= 1 and has(i - 1, NT):
                    keep_gT(ROUTED_BASE, i - 1, near - 1)

            running_counts()
            expert_tiles()
            token_rows()
            pipeline(dve, SHARED_FIRST, shared_run(0, 0, SHARED_FIRST))
            pipeline(dve, NT, routed)
            pipeline(dve, T - SHARED_FIRST, shared_run(SHARED_BASE, SHARED_FIRST, T - SHARED_FIRST))
            dve.wait_ge(y_read, SHARED_BASE + T - SHARED_FIRST)
            for k, tiles in enumerate(FINAL_PARTS):
                dve.wait_ge(gathered_in[k], 16 * (tiles.stop - tiles.start))
                dve.tensor_tensor(x_sb[:, tiles, :], gathered[:, tiles, :], x_sb[:, tiles, :], ALU.add
                                  ).then_inc(final_ready, 1)


_INS = ["L0_attn_x", "L0_attn_w_q", "L0_attn_w_k", "L0_attn_w_v", "L0_attn_w_o", "L0_ffn_router_DE",
        "L0_ffn_w1_eDF", "L0_ffn_w3_eDF", "L0_ffn_w2_eFD", "L0_ffn_ws1_DF", "L0_ffn_ws3_DF", "L0_ffn_ws2_FD"]
_OUTS = [((B, S, D), "float32")]


def kernel(**inputs):
    import numpy as np
    import concourse.bacc as bacc
    from concourse.bass_utils import run_bass_kernel_spmd as run

    nc = bacc.Bacc("TRN2", target_bir_lowering=False, num_devices=1)
    arrays, args = {}, []
    for name in _INS:
        a = np.ascontiguousarray(inputs[name])
        arrays[name] = a
        args.append(nc.dram_tensor(name, a.shape, mybir.dt.from_np(a.dtype), kind="ExternalInput").ap())
    outs = []
    for i, (shape, dtype) in enumerate(_OUTS):
        dt = mybir.dt.from_np(np.dtype(dtype))
        outs.append(nc.dram_tensor(f"out_{i}", shape, dt, kind="ExternalOutput").ap())
    preln_attention_moe_kernel(nc, *args, *outs)
    r = run(nc, [arrays], core_ids=[0])
    return r.results[0]["out_0"]
```
